# Optimizing a Trainium2 kernel written in Bass

```python
import numpy as np
import jax
import jax.numpy as jnp

def _softmax(x, axis=-1):
    return jax.nn.softmax(x, axis=axis)

def _gelu(x):
    return jax.nn.gelu(x, approximate=True)

def _silu(x):
    return jax.nn.silu(x)

def _sigmoid(x):
    return jax.nn.sigmoid(x)

def _layernorm(x, axis=-1, eps=1e-05):
    m = jnp.mean(x, axis=axis, keepdims=True)
    v = jnp.var(x, axis=axis, keepdims=True)
    return (x - m) / jnp.sqrt(v + eps)

def _scatter_add(tgt, idx, src, axis=0):
    return tgt.at[idx].add(src)

def _segment_sum(src, seg, n):
    return jax.ops.segment_sum(src, seg, n)
kernel_name = 'mk_adj_resnorm_d1_adj_r2_3b573a'

def setup_inputs(seed: int=0):
    np.random.seed(seed)
    _w = jnp.asarray

    def _rec_inputs():
        import jax
        import jax.numpy as jnp
        _gk = jax.random.key(seed)
        x = -0.0002144 + 1 * jax.random.normal(jax.random.fold_in(_gk, 1), (16, 512, 128), jnp.float32)
        _a = jax.random.bernoulli(jax.random.fold_in(_gk, 2), 0.0078125, (16, 512, 512))
        adj = _a.astype(jnp.int32)
        return (x, adj)
    x, adj = _rec_inputs()

    def _L0_gnn_setup():
        import jax, jax.numpy as jnp
        import numpy as np
        B, N, D, T = (256, 50, 128, 64)
        NEG = -9000000000000000.0
        LRELU_SLOPE = 0.2
        key = jax.random.key(seed)
        k0, k1, k2, k3, k4 = jax.random.split(key, 5)
        hidden = jax.random.normal(k0, (B, N, D), dtype=jnp.float32)
        adj = jax.random.randint(k1, (B, N, N), 0, 6, dtype=jnp.int32)
        A_interval = jax.random.uniform(k2, (B, N, N), dtype=jnp.float32)
        stdv = 1.0 / np.sqrt(D)
        a_rel = jax.random.uniform(k3, (5, D), dtype=jnp.float32, minval=-stdv, maxval=stdv)
        t_rel = jax.random.uniform(k4, (5, T), dtype=jnp.float32, minval=-stdv, maxval=stdv)
        time_w = jnp.asarray(1.0 / 10.0 ** np.linspace(0, 9, T, dtype=np.float32))
        return {'hidden': hidden, 'adj': adj, 'A_interval': A_interval, 'a_rel': a_rel, 't_rel': t_rel, 'time_w': time_w}
    _L0_gnn_all = _L0_gnn_setup()
    _L0_gnn_in = {k: v for k, v in _L0_gnn_all.items() if k in ('a_rel', 't_rel', 'time_w')}
    del _L0_gnn_all
    return {'x': x, 'adj': adj, 'L0_gnn_a_rel': _L0_gnn_in['a_rel'], 'L0_gnn_t_rel': _L0_gnn_in['t_rel'], 'L0_gnn_time_w': _L0_gnn_in['time_w']}

def reference(x, adj, L0_gnn_a_rel, L0_gnn_t_rel, L0_gnn_time_w):
    import jax
    import jax.numpy as jnp

    def _L0_gnn_ref(hidden, adj, A_interval, a_rel, t_rel, time_w):
        import jax, jax.numpy as jnp
        import numpy as np
        B, N, D, T = (256, 50, 128, 64)
        NEG = -9000000000000000.0
        LRELU_SLOPE = 0.2
        e_struct = jnp.einsum('bid,bjd,rd->bijr', hidden, hidden, a_rel)
        tenc = jax.lax.stop_gradient(jnp.cos(A_interval[..., None] * time_w))
        e_time = jnp.einsum('bijt,rt->bijr', tenc, t_rel)
        e = jax.nn.leaky_relu(e_struct + e_time, negative_slope=LRELU_SLOPE)
        idx = jnp.clip(adj - 1, 0, 4)[..., None]
        sel = jnp.take_along_axis(e, idx, axis=-1)[..., 0]
        alpha = jnp.where((adj >= 1) & (adj <= 5), sel, NEG)
        alpha = jax.nn.softmax(alpha, axis=-1)
        return jnp.einsum('bij,bjd->bid', alpha, hidden)
    x = _layernorm(x + _L0_gnn_ref(x, adj, adj, L0_gnn_a_rel, L0_gnn_t_rel, L0_gnn_time_w), axis=-1)
    return x

_drawn_inputs = setup_inputs


def setup_inputs(seed=0):
    import zlib

    import numpy as np

    out = dict(_drawn_inputs(seed))
    spreads = {}
    factors = {}
    for name, (base, spread) in spreads.items():
        noise = np.random.default_rng([zlib.crc32(name.encode()), seed]).standard_normal(out[name].shape)
        drawn = base * np.exp(spread * noise) if base else spread * noise
        out[name] = jnp.asarray(drawn.astype(out[name].dtype))
    for name, factor in factors.items():
        out[name] = (out[name] * factor).astype(out[name].dtype)
    return out
```

```python
import concourse.bass as bass
from concourse import mybir
from contextlib import ExitStack


def gnn_resnorm_kernel(
    nc: bass.Bass,
    x: bass.AP,
    adj: bass.AP,
    a_rel: bass.AP,
    t_rel: bass.AP,
    time_w: bass.AP,
    out: bass.AP,
):
    f32, bf16, i32, u8 = mybir.dt.float32, mybir.dt.bfloat16, mybir.dt.int32, mybir.dt.uint8
    ALU = mybir.AluOpType
    ACT = mybir.ActivationFunctionType
    AX = mybir.AxisListType

    B, N, D = x.shape
    R, T = t_rel.shape
    P = 128
    NT = N // P
    XBUF = 4
    NEG = -9000000000000000.0
    SLOPE = 0.2
    LIFT = (1.0 - SLOPE) / SLOPE
    EPS = 1e-5
    BIG = 2.0 ** 90
    SCORE_MAX = 1e15
    TWO_PI = 6.283185307179586
    PI_A = 6.28125
    PI_B = 0.0019350051879882812
    PI_C = TWO_PI - PI_A - PI_B
    ROUND = 1.5 * 2.0 ** 23

    x_v = x.rearrange("b (p t) d -> b p t d", t=NT)
    adj_v = adj.rearrange("b (p t) j -> b p t j", t=NT)
    out_v = out.rearrange("b (p t) d -> b p t d", t=NT)

    ctx = ExitStack()
    with ctx:
        def sb(name, shape, dt):
            return ctx.enter_context(nc.sbuf_tensor(name, shape, dt))

        def sem(name):
            return ctx.enter_context(nc.semaphore(name))

        ident = sb("ident", [P, P], f32)
        ones_col = sb("ones_col", [P, 1], f32)
        a_cols = sb("a_cols", [P, R], f32)
        a_scaled = sb("a_scaled", [P, 1], f32)
        w_row = sb("w_row", [P, T], f32)
        t_row = sb("t_row", [P, R * T], f32)
        theta = sb("theta", [P, R * T], f32)
        turns = sb("turns", [P, R * T], f32)
        c_rel = sb("c_rel", [P, R], f32)
        c_unit = sb("c_unit", [P, 1], f32)
        c_lift = sb("c_lift", [P, 1], f32)
        half_neg = sb("half_neg", [P, NT], f32)
        adj_sb = [sb(f"adj_sb{k}", [P, NT, N], i32) for k in range(XBUF)]
        x_sb = [sb(f"x_sb{k}", [P, NT, D], f32) for k in range(XBUF)]
        y_sb = [sb(f"y_sb{k}", [P, NT, D], f32) for k in range(XBUF)]
        mask_sb = [sb(f"mask_sb{k}", [P, NT, N], bf16) for k in range(2)]
        xT = [sb(f"xT{k}", [P, NT, P], f32) for k in range(2)]
        xaT = [sb(f"xaT{k}", [P, N], f32) for k in range(2)]
        e_sb = [sb(f"e_sb{k}", [P, NT, N], f32) for k in range(2)]
        p_sb = [sb(f"p_sb{k}", [P, NT, NT, P], f32) for k in range(2)]
        pT_sb = [sb(f"pT_sb{t}", [P, NT, P], f32) for t in range(NT)]
        row_max = [sb(f"row_max{k}", [P, NT], f32) for k in range(2)]
        row_max_all = sb("row_max_all", [P, B * NT], f32)
        lift = [sb(f"lift{h}", [P, NT // 2, N], f32) for h in range(NT // 2)]
        max_lift = sb("max_lift", [P, NT], f32)
        max_low = sb("max_low", [P, NT], f32)
        neg_max = [sb(f"neg_max{k}", [P, NT], f32) for k in range(2)]
        row_sum = [sb(f"row_sum{k}", [P, NT], f32) for k in range(2)]
        inv_sum = [sb(f"inv_sum{k}", [P, NT], f32) for k in range(2)]
        stats = [sb(f"stats{k}", [P, NT, 6], f32) for k in range(2)]
        mean_var = [sb(f"mean_var{k}", [P, NT, 2], f32) for k in range(2)]
        var_eps = [sb(f"var_eps{k}", [P, NT], f32) for k in range(2)]
        rstd = [sb(f"rstd{k}", [P, NT], f32) for k in range(2)]
        neg_mean = [sb(f"neg_mean{k}", [P, NT], f32) for k in range(2)]
        off_a = sb("off_a", [P, B * NT], f32)
        off_b = sb("off_b", [P, B * NT], f32)
        off_row = sb("off_row", [P, 1], f32)
        off_int = sb("off_int", [1, 1], i32)
        row_max2 = sb("row_max2", [P, NT], f32)
        hit = [sb(f"hit{k}", [P, N], u8) for k in range(2)]
        leaky = [sb(f"leaky{k}", [P, N], f32) for k in range(2)]
        e_k = [sb(f"e_k{k}", [P, N], f32) for k in range(2)]

        ring = [ctx.enter_context(nc.psum_tensor(f"ring{n}", [P, N], f32)) for n in range(NT)]
        pT_ps = [ctx.enter_context(nc.psum_tensor(f"pT_ps{k}", [P, NT, P], f32)) for k in range(2)]
        o_ps = [ctx.enter_context(nc.psum_tensor(f"o_ps{k}", [P, D], f32)) for k in range(2)]

        def score_bank(k, t):
            return ring[(k - 1 + t) % NT]

        def xT_bank(k):
            return ring[(k - 2) % NT][:].rearrange("p (t q) -> p t q", t=NT)

        const_in = sem("const_in")
        passed = sem("passed")
        x_in = [sem(f"x_in{k}") for k in range(XBUF)]
        adj_in = [sem(f"adj_in{k}") for k in range(XBUF)]
        stored = [sem(f"stored{k}") for k in range(XBUF)]
        ident_zero = sem("ident_zero")
        ident_ready = sem("ident_ready")
        angle_step = sem("angle_step")
        angle_ready = sem("angle_ready")
        cos_ready = sem("cos_ready")
        c_step = sem("c_step")
        c_ready = sem("c_ready")
        mask_ready = sem("mask_ready")
        xT_done = sem("xT_done")
        xT_ready = sem("xT_ready")
        score_done = sem("score_done")
        masked_ready = sem("masked_ready")
        lift_ready = sem("lift_ready")
        e_ready = sem("e_ready")
        max_parts = sem("max_parts")
        max_ready = sem("max_ready")
        p_ready = sem("p_ready")
        pT_done = sem("pT_done")
        pT_ready = sem("pT_ready")
        o_done = sem("o_done")
        inv_ready = sem("inv_ready")
        o_free = sem("o_free")
        stats_ready = sem("stats_ready")
        moments_ready = sem("moments_ready")
        var_ready = sem("var_ready")
        rstd_ready = sem("rstd_ready")
        y_ready = sem("y_ready")
        max_kept = sem("max_kept")
        off_step = sem("off_step")
        off_ready = sem("off_ready")
        off_sum = sem("off_sum")
        off_known = sem("off_known")
        g_in = sem("g_in")
        g_xT_done = sem("g_xT_done")
        g_xT_ready = sem("g_xT_ready")
        g_xa_ready = sem("g_xa_ready")
        g_score_done = sem("g_score_done")
        g_e_ready = sem("g_e_ready")
        g_hit = sem("g_hit")
        g_picked = sem("g_picked")
        g_fill = sem("g_fill")
        g_max = sem("g_max")
        g_neg_max = sem("g_neg_max")
        g_p_ready = sem("g_p_ready")
        g_pT_done = sem("g_pT_done")
        g_pT_ready = sem("g_pT_ready")
        g_o_done = sem("g_o_done")
        g_inv = sem("g_inv")
        g_y = sem("g_y")
        g_stats = sem("g_stats")
        g_moments = sem("g_moments")
        g_var = sem("g_var")
        g_rstd = sem("g_rstd")
        g_out = sem("g_out")
        g_stored = sem("g_stored")

        block = ctx.enter_context(nc.Block())

        LOOPED = B - XBUF

        def slots(engine, slot):
            slot(-1, 3, False, True, True)
            with engine.Fori(0, LOOPED // XBUF) as i:
                for k in range(XBUF):
                    slot(XBUF * i + k, k, True, True, True)
            for b in range(LOOPED, B):
                slot(b, b % XBUF, True, b + 1 < B, b + 2 < B)

        def turn(b, k):
            return 4 * (b - k)

        def plain_wait(engine, semaphore, value):
            engine.wait_ge(semaphore, value)
            engine.sem_inc(passed, 1)

        @block.sync
        def _(sp):
            def load_x(b, k):
                sp.dma_start(x_sb[k][:], x_v[bass.ds(b, 1)].rearrange("o p t d -> p (o t) d")).then_inc(x_in[k], 16)

            def load_adj(b, k):
                sp.dma_start(adj_sb[k][:], adj_v[bass.ds(b, 1)].rearrange("o p t j -> p (o t) j")).then_inc(adj_in[k], 16)

            load_x(0, 0)
            load_adj(0, 0)
            sp.dma_start(w_row[:], time_w[None, :].broadcast_to((P, T))).then_inc(const_in, 16)
            sp.dma_start(t_row[:], t_rel.rearrange("r t -> (r t)")[None, :].broadcast_to((P, R * T))).then_inc(const_in, 16)
            with nc.allow_non_contiguous_dma(reason="five short columns"):
                sp.dma_start(a_cols[:], a_rel.rearrange("r d -> d r")).then_inc(const_in, 16)
            for k in range(1, XBUF):
                load_x(k, k)
                load_adj(k, k)
            for k in range(XBUF):
                sp.sem_inc(stored[k], 16)

            def store(b, k):
                plain_wait(sp, y_ready, NT * b + NT)
                sp.dma_start(out_v[bass.ds(b, 1)].rearrange("o p t d -> p (o t) d"), y_sb[k][:]).then_inc(stored[k], 16)

            with sp.Fori(0, LOOPED // XBUF) as i:
                for k in range(XBUF):
                    b = XBUF * i + k
                    plain_wait(sp, mask_ready, b + 1)
                    load_adj(b + XBUF, k)
                    plain_wait(sp, o_free, NT * b + 2 * NT)
                    load_x(b + XBUF, k)
                    store(b, k)
            for b in range(LOOPED, B):
                store(b, b % XBUF)
            for k in range(XBUF):
                sp.wait_ge(stored[k], 16 * (B // XBUF + 1))

            sp.wait_ge(off_known, 1)
            off = sp.value_load(off_int[0:1, 0:1], min_val=0, max_val=P)
            with sp.If(off > 0):
                with sp.Fori(0, B, 1) as b:
                    sp.dma_start(x_sb[0][:], x_v[bass.ds(b, 1)].rearrange("o p t d -> p (o t) d")).then_inc(g_in, 16)
                    sp.dma_start(adj_sb[0][:], adj_v[bass.ds(b, 1)].rearrange("o p t j -> p (o t) j")).then_inc(g_in, 16)
                    plain_wait(sp, g_out, NT * b + NT)
                    sp.dma_start(out_v[bass.ds(b, 1)].rearrange("o p t d -> p (o t) d"), y_sb[0][:]).then_inc(g_stored, 16)
                    plain_wait(sp, g_stored, 16 * b + 16)

        @block.gpsimd
        def _(pool):
            nc.gpsimd.memset(ident[:], 0.0).then_inc(ident_zero, 1)
            nc.gpsimd.memset(half_neg[:], -0.5).then_inc(ident_zero, 1)
            pool.wait_ge(ident_zero, 2)
            nc.gpsimd.affine_select(out=ident[:], in_=ident[:], compare_op=ALU.not_equal, fill=1.0, base=0,
                                    pattern=[[-1, P]], channel_multiplier=1).then_inc(ident_ready, 1)

            def normalise(k2, y, moments, moments_at, var, var_at, root, root_at, done):
                plain_wait(pool, moments, moments_at)
                nc.gpsimd.tensor_scalar(var_eps[k2][:], mean_var[k2][:, :, 1], EPS, None, ALU.add).then_inc(var, 1)
                nc.gpsimd.tensor_scalar(neg_mean[k2][:], mean_var[k2][:, :, 0], -1.0, None, ALU.mult).then_inc(var, 1)
                pool.wait_ge(var, var_at)
                nc.gpsimd.tensor_tensor(rstd[k2][:], var_eps[k2][:], half_neg[:], ALU.pow).then_inc(root, 1)
                plain_wait(pool, root, root_at)
                for t in range(NT):
                    nc.gpsimd.tensor_scalar(y[:, t, :], y[:, t, :], neg_mean[k2][:, t:t + 1], rstd[k2][:, t:t + 1],
                                            ALU.add, ALU.mult).then_inc(done, 1)

            def lift_scores(b, k2):
                for h in range(NT // 2):
                    pool.wait_ge(lift_ready, 2 * b + h + 1)
                    e = e_sb[k2][:, 2 * h:2 * h + 2, :]
                    nc.gpsimd.tensor_tensor(e, e, lift[h][:], ALU.add).then_inc(e_ready, 1)

            def slot(b, k, here, next1, next2):
                if next1:
                    lift_scores(b + 1, (k + 1) % 2)
                    pool.wait_ge(masked_ready, NT * b + 2 * NT)
                    nc.gpsimd.tensor_copy(row_max_all[:, bass.ds(NT * b + NT, NT)],
                                          row_max[(k + 1) % 2][:]).then_inc(max_kept, 1)
                if here:
                    normalise(k % 2, y_sb[k], moments_ready, NT * b + NT, var_ready, 2 * b + 2,
                              rstd_ready, b + 1, y_ready)

            slots(pool, slot)

            pool.wait_ge(off_known, 1)
            off = pool.value_load(off_int[0:1, 0:1], min_val=0, max_val=P)
            with pool.If(off > 0):
                with pool.Fori(0, B, 1) as b:
                    normalise(0, y_sb[0], g_moments, NT * b + NT, g_var, 2 * b + 2, g_rstd, b + 1, g_out)

        @block.tensor
        def _(pe):
            def transpose_x(b, k):
                pe.wait_ge(x_in[k], turn(b, k) + 16)
                if not isinstance(b, int) or b > 0:
                    pe.wait_ge(masked_ready, NT * b - NT + 1)
                for t in range(NT):
                    last = nc.tensor.transpose(xT_bank(k)[:, t, :], x_sb[k][:, t, :], ident[:])
                last.then_inc(xT_done, 1)

            def score(b, k, t):
                if t == 0:
                    pe.wait_ge(xT_ready, 2 * b + 2)
                if t < NT - 1 and (not isinstance(b, int) or b > 0):
                    pe.wait_ge(masked_ready, NT * b + t + 2 - NT)
                nc.tensor.matmul(score_bank(k, t)[:], xT[k % 2][:, t, :], xaT[k % 2][:],
                                 start=True, stop=True).then_inc(score_done, 1)

            def transpose_p(b, k2, t):
                pe.wait_ge(p_ready, NT * b + t + 1)
                for c in range(NT):
                    last = nc.tensor.transpose(pT_ps[t % 2][:, c, :], p_sb[k2][:, t, c, :], ident[:])
                last.then_inc(pT_done, 1)

            def weigh(b, k, t):
                pe.wait_ge(pT_ready, NT * b + t + 1)
                pe.wait_ge(o_free, NT * b + t + NT - 1)
                for c in range(NT):
                    last = nc.tensor.matmul(o_ps[t % 2][:], pT_sb[t][:, c, :], x_sb[k][:, c, :],
                                            start=(c == 0), stop=(c == NT - 1))
                last.then_inc(o_done, 1)

            def slot(b, k, here, next1, next2):
                for t in range(NT):
                    if next1:
                        score(b + 1, (k + 1) % XBUF, t)
                    if here:
                        transpose_p(b, k % 2, t)
                        if t > 0:
                            weigh(b, k, t - 1)
                if next2:
                    transpose_x(b + 2, (k + 2) % XBUF)
                if here:
                    weigh(b, k, NT - 1)

            pe.wait_ge(ident_ready, 1)
            transpose_x(0, 0)
            slots(pe, slot)

            pe.wait_ge(off_ready, 2)
            nc.tensor.matmul(ring[0][0:1, 0:1], off_row[:], ones_col[:], start=True, stop=True).then_inc(off_sum, 1)
            pe.wait_ge(off_known, 1)
            off = pe.value_load(off_int[0:1, 0:1], min_val=0, max_val=P)
            with pe.If(off > 0):
                with pe.Fori(0, B, 1) as b:
                    pe.wait_ge(g_in, 32 * b + 32)
                    for t in range(NT):
                        last = nc.tensor.transpose(xT_bank(2)[:, t, :], x_sb[0][:, t, :], ident[:])
                    last.then_inc(g_xT_done, 1)
                    for r in range(R):
                        pe.wait_ge(g_xT_ready, b + 1)
                        pe.wait_ge(g_xa_ready, R * b + r + 1)
                        for t in range(NT):
                            if r > 0:
                                pe.wait_ge(g_e_ready, R * NT * b + NT * (r - 1) + t + 1)
                            nc.tensor.matmul(ring[t][:], xT[0][:, t, :], xaT[r % 2][:],
                                             start=True, stop=True).then_inc(g_score_done, 1)
                    for t in range(NT):
                        pe.wait_ge(g_p_ready, NT * b + t + 1)
                        for c in range(NT):
                            last = nc.tensor.transpose(pT_ps[t % 2][:, c, :], p_sb[0][:, t, c, :], ident[:])
                        last.then_inc(g_pT_done, 1)
                        pe.wait_ge(g_pT_ready, NT * b + t + 1)
                        if t >= 2:
                            pe.wait_ge(g_y, NT * b + t - 1)
                        for c in range(NT):
                            last = nc.tensor.matmul(o_ps[t % 2][:], pT_sb[t][:, c, :], x_sb[0][:, c, :],
                                                    start=(c == 0), stop=(c == NT - 1))
                        last.then_inc(g_o_done, 1)

        @block.scalar
        def _(act):
            act.wait_ge(angle_ready, 1)
            nc.scalar.activation(turns[:], theta[:], ACT.Sin).then_inc(cos_ready, 1)
            act.wait_ge(c_ready, 3)

            def exponents(b, k2, h):
                act.wait_ge(masked_ready, NT * b + 2 * h + 2)
                nc.scalar.activation(lift[h][:], e_sb[k2][:, 2 * h:2 * h + 2, :], ACT.Relu, bias=c_lift[:],
                                     scale=LIFT).then_inc(lift_ready, 1)
                act.wait_ge(e_ready, 2 * b + h + 1)
                act.wait_ge(max_ready, 2 * b + h + 1)
                for t in (2 * h, 2 * h + 1):
                    nc.scalar.activation(p_sb[k2][:, t, :, :], e_sb[k2][:, t, :].rearrange("p (q c) -> p c q", c=NT),
                                         ACT.Exp, bias=neg_max[k2][:, t:t + 1], scale=SLOPE * BIG,
                                         accum_out=row_sum[k2][:, t:t + 1]).then_inc(p_ready, 1)

            def copy_pT(b, t):
                act.wait_ge(pT_done, NT * b + t + 1)
                nc.scalar.copy(pT_sb[t][:], pT_ps[t % 2][:]).then_inc(pT_ready, 1)

            def slot(b, k, here, next1, next2):
                for h in range(NT // 2):
                    if here:
                        copy_pT(b, 2 * h)
                        copy_pT(b, 2 * h + 1)
                    if next1:
                        exponents(b + 1, (k + 1) % 2, h)

            slots(act, slot)

            act.wait_ge(off_known, 1)
            off = act.value_load(off_int[0:1, 0:1], min_val=0, max_val=P)
            with act.If(off > 0):
                with act.Fori(0, B, 1) as b:
                    for u in range(R * NT):
                        r, t = divmod(u, NT)
                        act.wait_ge(g_score_done, R * NT * b + u + 1)
                        if u >= 2:
                            act.wait_ge(g_picked, R * NT * b + u - 1)
                        nc.scalar.activation(e_k[u % 2][:], ring[t][:], ACT.Identity,
                                             bias=c_rel[:, r:r + 1]).then_inc(g_e_ready, 1)
                    for t in range(NT):
                        act.wait_ge(g_neg_max, NT * b + t + 1)
                        nc.scalar.activation(p_sb[0][:, t, :, :], e_sb[0][:, t, :].rearrange("p (q c) -> p c q", c=NT),
                                             ACT.Exp, bias=neg_max[0][:, t:t + 1],
                                             accum_out=row_sum[0][:, t:t + 1]).then_inc(g_p_ready, 1)
                        act.wait_ge(g_pT_done, NT * b + t + 1)
                        nc.scalar.copy(pT_sb[t][:], pT_ps[t % 2][:]).then_inc(g_pT_ready, 1)

        @block.vector
        def _(dve):
            steps = [0]

            def angle(ins):
                steps[0] += 1
                ins.then_inc(angle_step, 1)
                dve.wait_ge(angle_step, steps[0])

            nc.vector.memset(ones_col[:], 1.0).then_inc(off_ready, 1)
            dve.sem_inc(o_free, NT)

            def constants():
                dve.wait_ge(const_in, 48)
                for r in range(R):
                    last = nc.vector.tensor_scalar(theta[:, r * T:(r + 1) * T], w_row[:], float(r + 1), None, ALU.mult)
                    if r < R - 1:
                        last.then_inc(angle_step, 1)
                        steps[0] += 1
                angle(last)
                angle(nc.vector.tensor_scalar(turns[:], theta[:], 1.0 / TWO_PI, ROUND, ALU.mult, ALU.add))
                angle(nc.vector.tensor_scalar(turns[:], turns[:], -ROUND, None, ALU.add))
                for part in (PI_A, PI_B, PI_C):
                    angle(nc.vector.scalar_tensor_tensor(theta[:], turns[:], -part, theta[:], ALU.mult, ALU.add))
                angle(nc.vector.scalar_tensor_tensor(turns[:], theta[:], -1.0, theta[:], ALU.mult, ALU.max))
                nc.vector.tensor_scalar(theta[:], turns[:], -1.0, TWO_PI / 4, ALU.mult, ALU.add).then_inc(angle_ready, 1)
                nc.vector.tensor_scalar(a_scaled[:], a_cols[:, 0:1], 1.0 / BIG, None, ALU.mult).then_inc(c_step, 1)
                dve.wait_ge(cos_ready, 1)
                nc.vector.tensor_tensor(turns[:], turns[:], t_row[:], ALU.mult).then_inc(c_step, 1)
                dve.wait_ge(c_step, 2)
                nc.vector.reduce_sum(c_rel[:], turns[:].rearrange("p (r t) -> p r t", t=T), axis=AX.X).then_inc(c_ready, 1)
                dve.wait_ge(c_ready, 1)
                nc.vector.tensor_scalar(c_unit[:], c_rel[:, 0:1], 1.0 / BIG, None, ALU.mult).then_inc(c_ready, 1)
                nc.vector.tensor_scalar(c_lift[:], c_rel[:, 0:1], LIFT / BIG, None, ALU.mult).then_inc(c_ready, 1)
                dve.wait_ge(c_ready, 3)

            def make_mask(b, k):
                dve.wait_ge(adj_in[k], turn(b, k) + 16)
                nc.vector.tensor_scalar(mask_sb[k % 2][:], adj_sb[k][:], 0.0, -1.0, ALU.max, ALU.add).then_inc(mask_ready, 1)

            def copy_xT(b, k):
                dve.wait_ge(xT_done, b + 1)
                nc.vector.tensor_copy(xT[k % 2][:], xT_bank(k)).then_inc(xT_ready, 1)
                nc.vector.tensor_scalar(xaT[k % 2][:].rearrange("d (p t) -> d t p", t=NT), xT_bank(k), a_scaled[:], None,
                                        ALU.mult).then_inc(xT_ready, 1)

            def mask_scores(b, k, t):
                k2 = k % 2
                if t == 0:
                    dve.wait_ge(mask_ready, b + 1)
                    if not isinstance(b, int) or b >= 2:
                        dve.wait_ge(max_kept, b)
                plain_wait(dve, score_done, NT * b + t + 1)
                nc.vector.tensor_tensor_reduce(out=e_sb[k2][:, t, :], in0=score_bank(k, t)[:], in1=mask_sb[k2][:, t, :],
                                               scale=1.0, scalar=-3.0e38, op0=ALU.add, op1=ALU.max,
                                               accum_out=row_max[k2][:, t:t + 1]).then_inc(masked_ready, 1)

            def negate_maxima(b, k2, h):
                cols = slice(2 * h, 2 * h + 2)
                dve.wait_ge(masked_ready, NT * b + 2 * h + 2)
                nc.vector.tensor_scalar(max_lift[:, cols], row_max[k2][:, cols], c_unit[:], 0.0,
                                        ALU.add, ALU.max).then_inc(max_parts, 1)
                nc.vector.tensor_scalar(max_low[:, cols], row_max[k2][:, cols], -SLOPE * BIG, None,
                                        ALU.mult).then_inc(max_parts, 1)
                dve.wait_ge(max_parts, 4 * b + 2 * h + 2)
                nc.vector.scalar_tensor_tensor(neg_max[k2][:, cols], max_lift[:, cols], -SLOPE * LIFT * BIG,
                                               max_low[:, cols], ALU.mult, ALU.add).then_inc(max_ready, 1)

            def invert_sums(b, k):
                dve.wait_ge(p_ready, NT * b + NT)
                nc.vector.reciprocal(inv_sum[k % 2][:], row_sum[k % 2][:]).then_inc(inv_ready, 1)
                dve.wait_ge(stored[k], turn(b, k) + 16)
                dve.wait_ge(inv_ready, b + 1)

            def add_residual(b, k, t):
                dve.wait_ge(o_done, NT * b + t + 1)
                nc.vector.scalar_tensor_tensor(y_sb[k][:, t, :], o_ps[t % 2][:], inv_sum[k % 2][:, t:t + 1],
                                               x_sb[k][:, t, :], ALU.mult, ALU.add).then_inc(o_free, 1)

            def moments(b, k):
                for t in range(NT):
                    dve.wait_ge(o_free, NT * b + NT + t + 1)
                    nc.vector.bn_stats(stats[k % 2][:, t, :], y_sb[k][:, t, :]).then_inc(stats_ready, 1)
                plain_wait(dve, stats_ready, NT * b + NT)
                for t in range(NT):
                    nc.vector.bn_aggr(mean_var[k % 2][:, t, :], stats[k % 2][:, t, :]).then_inc(moments_ready, 1)

            def slot(b, k, here, next1, next2):
                for t in range(NT):
                    if next1:
                        mask_scores(b + 1, (k + 1) % XBUF, t)
                        if t % 2 == 1:
                            negate_maxima(b + 1, (k + 1) % 2, t // 2)
                    if next2 and t == 0:
                        make_mask(b + 2, (k + 2) % XBUF)
                    if here and t == 1:
                        invert_sums(b, k)
                    if here and t >= 2:
                        add_residual(b, k, t - 2)
                if next2:
                    copy_xT(b + 2, (k + 2) % XBUF)
                if here:
                    add_residual(b, k, 2)
                    add_residual(b, k, 3)
                    moments(b, k)

            constants()
            dve.wait_ge(c_step, 1)
            copy_xT(0, 0)
            make_mask(0, 0)
            slots(dve, slot)

            dve.wait_ge(max_kept, B)
            nc.vector.tensor_scalar(off_a[:], row_max_all[:], -0.5, None, ALU.is_gt).then_inc(off_step, 1)
            dve.wait_ge(off_step, 1)
            nc.vector.scalar_tensor_tensor(off_b[:], row_max_all[:], -SCORE_MAX / BIG, off_a[:], ALU.is_lt,
                                           ALU.mult).then_inc(off_step, 1)
            dve.wait_ge(off_step, 2)
            nc.vector.scalar_tensor_tensor(off_a[:], row_max_all[:], SCORE_MAX / BIG, off_b[:], ALU.is_gt,
                                           ALU.add).then_inc(off_step, 1)
            dve.wait_ge(off_step, 3)
            nc.vector.reduce_max(off_row[:], off_a[:], axis=AX.X).then_inc(off_ready, 1)
            dve.wait_ge(off_sum, 1)
            nc.vector.tensor_copy(off_int[:], ring[0][0:1, 0:1]).then_inc(off_known, 1)
            dve.wait_ge(off_known, 1)
            off = dve.value_load(off_int[0:1, 0:1], min_val=0, max_val=P)
            with dve.If(off > 0):
                with dve.Fori(0, B, 1) as b:
                    nc.vector.memset(e_sb[0][:], NEG).then_inc(g_fill, 1)
                    dve.wait_ge(g_xT_done, b + 1)
                    nc.vector.tensor_copy(xT[0][:], xT_bank(2)).then_inc(g_xT_ready, 1)
                    dve.wait_ge(g_xT_ready, b + 1)
                    dve.wait_ge(g_in, 32 * b + 32)
                    dve.wait_ge(g_fill, b + 1)
                    for r in range(R):
                        if r >= 2:
                            dve.wait_ge(g_score_done, R * NT * b + NT * (r - 1))
                        nc.vector.tensor_scalar(xaT[r % 2][:].rearrange("d (p t) -> d t p", t=NT), xT[0][:],
                                                a_cols[:, r:r + 1], None, ALU.mult).then_inc(g_xa_ready, 1)
                        for t in range(NT):
                            u = NT * r + t
                            nc.vector.tensor_scalar(hit[u % 2][:], adj_sb[0][:, t, :], float(r + 1), None,
                                                    ALU.is_equal).then_inc(g_hit, 1)
                            dve.wait_ge(g_e_ready, R * NT * b + u + 1)
                            nc.vector.scalar_tensor_tensor(leaky[u % 2][:], e_k[u % 2][:], SLOPE, e_k[u % 2][:],
                                                           ALU.mult, ALU.max).then_inc(g_hit, 1)
                            plain_wait(dve, g_hit, 2 * (R * NT * b + u) + 2)
                            nc.vector.copy_predicated(e_sb[0][:, t, :], hit[u % 2][:], leaky[u % 2][:]).then_inc(g_picked, 1)
                    for t in range(NT):
                        dve.wait_ge(g_picked, R * NT * b + NT * (R - 1) + t + 1)
                        nc.vector.reduce_max(row_max2[:, t:t + 1], e_sb[0][:, t, :], axis=AX.X).then_inc(g_max, 1)
                        dve.wait_ge(g_max, NT * b + t + 1)
                        nc.vector.tensor_scalar(neg_max[0][:, t:t + 1], row_max2[:, t:t + 1], -1.0, None,
                                                ALU.mult).then_inc(g_neg_max, 1)
                    dve.wait_ge(g_p_ready, NT * b + NT)
                    nc.vector.reciprocal(inv_sum[0][:], row_sum[0][:]).then_inc(g_inv, 1)
                    dve.wait_ge(g_inv, b + 1)
                    for t in range(NT):
                        dve.wait_ge(g_o_done, NT * b + t + 1)
                        nc.vector.scalar_tensor_tensor(y_sb[0][:, t, :], o_ps[t % 2][:], inv_sum[0][:, t:t + 1],
                                                       x_sb[0][:, t, :], ALU.mult, ALU.add).then_inc(g_y, 1)
                        dve.wait_ge(g_y, NT * b + t + 1)
                        nc.vector.bn_stats(stats[0][:, t, :], y_sb[0][:, t, :]).then_inc(g_stats, 1)
                        plain_wait(dve, g_stats, NT * b + t + 1)
                        nc.vector.bn_aggr(mean_var[0][:, t, :], stats[0][:, t, :]).then_inc(g_moments, 1)


_INS = ["x", "adj", "L0_gnn_a_rel", "L0_gnn_t_rel", "L0_gnn_time_w"]


def kernel(**inputs):
    import numpy as _np
    import concourse.bacc as _bacc
    from concourse import mybir as _mybir
    from concourse.bass_utils import run_bass_kernel_spmd as _run

    nc = _bacc.Bacc("TRN2", target_bir_lowering=False, num_devices=1)
    arrays, args = {}, []
    for name in _INS:
        a = _np.ascontiguousarray(inputs[name])
        arrays[f"in_{name}_dram"] = a
        args.append(nc.dram_tensor(f"in_{name}_dram", a.shape, _mybir.dt.from_np(a.dtype), kind="ExternalInput").ap())
    shape = inputs["x"].shape
    args.append(nc.dram_tensor("out_0_dram", shape, _mybir.dt.float32, kind="ExternalOutput").ap())
    gnn_resnorm_kernel(nc, *args)
    r = _run(nc, [arrays], core_ids=[0])
    return r.results[0]["out_0_dram"]
```

```python
import concourse.bass as bass
from concourse import mybir
from contextlib import ExitStack


def gnn_resnorm_kernel(
    nc: bass.Bass,
    x: bass.AP,
    adj: bass.AP,
    a_rel: bass.AP,
    t_rel: bass.AP,
    time_w: bass.AP,
    out: bass.AP,
):
    f32, bf16, i32, u8 = mybir.dt.float32, mybir.dt.bfloat16, mybir.dt.int32, mybir.dt.uint8
    ALU = mybir.AluOpType
    ACT = mybir.ActivationFunctionType
    AX = mybir.AxisListType

    B, N, D = x.shape
    R, T = t_rel.shape
    P = 128
    NT = N // P
    XBUF = 4
    NEG = -9000000000000000.0
    SLOPE = 0.2
    EPS = 1e-5
    BIG = 2.0 ** 90
    SCORE_MAX = 1e15
    TWO_PI = 6.283185307179586
    PI_A = 6.28125
    PI_B = 0.0019350051879882812
    PI_C = TWO_PI - PI_A - PI_B
    ROUND = 1.5 * 2.0 ** 23

    x_v = x.rearrange("b (p t) d -> b p t d", t=NT)
    adj_v = adj.rearrange("b (p t) j -> b p t j", t=NT)
    out_v = out.rearrange("b (p t) d -> b p t d", t=NT)

    ctx = ExitStack()
    with ctx:
        def sb(name, shape, dt):
            return ctx.enter_context(nc.sbuf_tensor(name, shape, dt))

        def sem(name):
            return ctx.enter_context(nc.semaphore(name))

        ident = sb("ident", [P, P], f32)
        ones_col = sb("ones_col", [P, 1], f32)
        a_cols = sb("a_cols", [P, R], f32)
        a_scaled = sb("a_scaled", [P, 1], f32)
        w_row = sb("w_row", [P, T], f32)
        t_row = sb("t_row", [P, R * T], f32)
        theta = sb("theta", [P, R * T], f32)
        turns = sb("turns", [P, R * T], f32)
        c_rel = sb("c_rel", [P, R], f32)
        c_unit = sb("c_unit", [P, 1], f32)
        half_neg = sb("half_neg", [P, NT], f32)
        adj_sb = [sb(f"adj_sb{k}", [P, NT, N], i32) for k in range(XBUF)]
        x_sb = [sb(f"x_sb{k}", [P, NT, D], f32) for k in range(XBUF)]
        y_sb = [sb(f"y_sb{k}", [P, NT, D], f32) for k in range(XBUF)]
        mask_sb = [sb(f"mask_sb{k}", [P, NT, N], f32) for k in range(2)]
        xT = [sb(f"xT{k}", [P, NT, P], f32) for k in range(2)]
        xaT = [sb(f"xaT{k}", [P, N], f32) for k in range(2)]
        e_sb = [sb(f"e_sb{k}", [P, NT, N], f32) for k in range(2)]
        p_sb = [sb(f"p_sb{k}", [P, NT, NT, P], f32) for k in range(2)]
        pT_sb = [sb(f"pT_sb{t}", [P, NT, P], f32) for t in range(NT)]
        row_max = [sb(f"row_max{k}", [P, NT], f32) for k in range(2)]
        row_max_all = sb("row_max_all", [P, B * NT], f32)
        max_leaky = sb("max_leaky", [P, NT], f32)
        neg_max = [sb(f"neg_max{k}", [P, NT], f32) for k in range(2)]
        row_sum = [sb(f"row_sum{k}", [P, NT], f32) for k in range(2)]
        inv_sum = [sb(f"inv_sum{k}", [P, NT], f32) for k in range(XBUF)]
        inv_sum_all = sb("inv_sum_all", [P, B * NT], f32)
        stats = [sb(f"stats{k}", [P, NT, 6], f32) for k in range(XBUF)]
        mean_var = [sb(f"mean_var{k}", [P, NT, 2], f32) for k in range(XBUF)]
        var_eps = [sb(f"var_eps{k}", [P, NT], f32) for k in range(XBUF)]
        rstd = [sb(f"rstd{k}", [P, NT], f32) for k in range(XBUF)]
        neg_mean = [sb(f"neg_mean{k}", [P, NT], f32) for k in range(XBUF)]
        off_a = sb("off_a", [P, B * NT], f32)
        off_b = sb("off_b", [P, B * NT], f32)
        off_c = sb("off_c", [P, B * NT], f32)
        off_row = sb("off_row", [P, 1], f32)
        off_int = sb("off_int", [1, 1], i32)
        row_max2 = sb("row_max2", [P, NT], f32)
        hit = [sb(f"hit{k}", [P, N], u8) for k in range(2)]
        leaky = [sb(f"leaky{k}", [P, N], f32) for k in range(2)]
        e_k = [sb(f"e_k{k}", [P, N], f32) for k in range(2)]

        ring = [ctx.enter_context(nc.psum_tensor(f"ring{n}", [P, N], f32)) for n in range(NT)]
        pT_ps = [ctx.enter_context(nc.psum_tensor(f"pT_ps{k}", [P, NT, P], f32)) for k in range(2)]
        o_ps = [ctx.enter_context(nc.psum_tensor(f"o_ps{k}", [P, D], f32)) for k in range(2)]

        def score_bank(k, t):
            return ring[(k - 1 + t + (t >= NT // 2)) % NT]

        def xT_bank(k):
            return ring[k % NT][:].rearrange("p (t q) -> p t q", t=NT)

        const_in = sem("const_in")
        a_in = sem("a_in")
        a_ready = sem("a_ready")
        passed = sem("passed")
        x_in = [sem(f"x_in{k}") for k in range(XBUF)]
        adj_in = [sem(f"adj_in{k}") for k in range(XBUF)]
        stored = [sem(f"stored{k}") for k in range(XBUF)]
        ident_zero = sem("ident_zero")
        ident_ready = sem("ident_ready")
        angle_step = sem("angle_step")
        angle_ready = sem("angle_ready")
        cos_ready = sem("cos_ready")
        c_step = sem("c_step")
        c_ready = sem("c_ready")
        mask_ready = sem("mask_ready")
        xT_done = sem("xT_done")
        xT_ready = sem("xT_ready")
        score_done = sem("score_done")
        masked_ready = sem("masked_ready")
        e_ready = sem("e_ready")
        max_leaky_ready = sem("max_leaky_ready")
        max_ready = sem("max_ready")
        p_ready = sem("p_ready")
        pT_done = sem("pT_done")
        pT_ready = sem("pT_ready")
        o_done = sem("o_done")
        inv_ready = sem("inv_ready")
        o_free = sem("o_free")
        stats_ready = sem("stats_ready")
        moments_ready = sem("moments_ready")
        var_ready = sem("var_ready")
        rstd_ready = sem("rstd_ready")
        y_ready = sem("y_ready")
        max_kept = sem("max_kept")
        sum_kept = sem("sum_kept")
        off_step = sem("off_step")
        off_ready = sem("off_ready")
        off_sum = sem("off_sum")
        off_known = sem("off_known")
        g_in = sem("g_in")
        g_xT_done = sem("g_xT_done")
        g_xT_ready = sem("g_xT_ready")
        g_xa_ready = sem("g_xa_ready")
        g_score_done = sem("g_score_done")
        g_e_ready = sem("g_e_ready")
        g_hit = sem("g_hit")
        g_picked = sem("g_picked")
        g_fill = sem("g_fill")
        g_max = sem("g_max")
        g_neg_max = sem("g_neg_max")
        g_p_ready = sem("g_p_ready")
        g_pT_done = sem("g_pT_done")
        g_pT_ready = sem("g_pT_ready")
        g_o_done = sem("g_o_done")
        g_inv = sem("g_inv")
        g_y = sem("g_y")
        g_stats = sem("g_stats")
        g_moments = sem("g_moments")
        g_var = sem("g_var")
        g_rstd = sem("g_rstd")
        g_out = sem("g_out")
        g_stored = sem("g_stored")

        block = ctx.enter_context(nc.Block())

        LOOPED = B - XBUF

        def slots(engine, slot):
            slot(-1, 3, False, True, True)
            with engine.Fori(0, LOOPED // XBUF) as i:
                for k in range(XBUF):
                    slot(XBUF * i + k, k, True, True, True)
            for b in range(LOOPED, B):
                slot(b, b % XBUF, True, b + 1 < B, b + 2 < B)

        def turn(b, k):
            return 4 * (b - k)

        def plain_wait(engine, semaphore, value):
            engine.wait_ge(semaphore, value)
            engine.sem_inc(passed, 1)

        @block.sync
        def _(sp):
            def load_x(b, k):
                sp.dma_start(x_sb[k][:], x_v[bass.ds(b, 1)].rearrange("o p t d -> p (o t) d")).then_inc(x_in[k], 16)

            def load_adj(b, k):
                sp.dma_start(adj_sb[k][:], adj_v[bass.ds(b, 1)].rearrange("o p t j -> p (o t) j")).then_inc(adj_in[k], 16)

            load_x(0, 0)
            load_adj(0, 0)
            for k in range(1, XBUF):
                load_x(k, k)
                load_adj(k, k)
            for k in range(XBUF):
                sp.sem_inc(stored[k], 16)

            def store(b, k):
                plain_wait(sp, y_ready, NT * b + NT)
                sp.dma_start(out_v[bass.ds(b, 1)].rearrange("o p t d -> p (o t) d"), y_sb[k][:]).then_inc(stored[k], 16)

            with sp.Fori(0, LOOPED // XBUF) as i:
                for k in range(XBUF):
                    b = XBUF * i + k
                    plain_wait(sp, mask_ready, b + 1)
                    load_adj(b + XBUF, k)
                    plain_wait(sp, o_free, NT * b + 2 * NT)
                    load_x(b + XBUF, k)
                    store(b, k)
            for b in range(LOOPED, B):
                store(b, b % XBUF)
            for k in range(XBUF):
                sp.wait_ge(stored[k], 16 * (B // XBUF + 1))

            sp.wait_ge(off_known, 1)
            off = sp.value_load(off_int[0:1, 0:1], min_val=0, max_val=P)
            with sp.If(off > 0):
                with sp.Fori(0, B, 1) as b:
                    sp.dma_start(x_sb[0][:], x_v[bass.ds(b, 1)].rearrange("o p t d -> p (o t) d")).then_inc(g_in, 16)
                    sp.dma_start(adj_sb[0][:], adj_v[bass.ds(b, 1)].rearrange("o p t j -> p (o t) j")).then_inc(g_in, 16)
                    plain_wait(sp, g_out, NT * b + NT)
                    sp.dma_start(out_v[bass.ds(b, 1)].rearrange("o p t d -> p (o t) d"), y_sb[0][:]).then_inc(g_stored, 16)
                    plain_wait(sp, g_stored, 16 * b + 16)

        @block.gpsimd
        def _(pool):
            nc.gpsimd.memset(ident[:], 0.0).then_inc(ident_zero, 1)
            nc.gpsimd.memset(half_neg[:], -0.5).then_inc(ident_zero, 1)
            pool.wait_ge(ident_zero, 2)
            nc.gpsimd.affine_select(out=ident[:], in_=ident[:], compare_op=ALU.not_equal, fill=1.0, base=0,
                                    pattern=[[-1, P]], channel_multiplier=1).then_inc(ident_ready, 1)

            def normalise(k, y, moments, moments_at, var, var_at, root, root_at, done):
                plain_wait(pool, moments, moments_at)
                nc.gpsimd.tensor_scalar(var_eps[k][:], mean_var[k][:, :, 1], EPS, None, ALU.add).then_inc(var, 1)
                nc.gpsimd.tensor_scalar(neg_mean[k][:], mean_var[k][:, :, 0], -1.0, None, ALU.mult).then_inc(var, 1)
                pool.wait_ge(var, var_at)
                nc.gpsimd.tensor_tensor(rstd[k][:], var_eps[k][:], half_neg[:], ALU.pow).then_inc(root, 1)
                plain_wait(pool, root, root_at)
                for t in range(NT):
                    nc.gpsimd.tensor_scalar(y[:, t, :], y[:, t, :], neg_mean[k][:, t:t + 1], rstd[k][:, t:t + 1],
                                            ALU.add, ALU.mult).then_inc(done, 1)

            def slot(b, k, here, next1, next2):
                if next1:
                    pool.wait_ge(masked_ready, NT * b + 2 * NT)
                    nc.gpsimd.tensor_copy(row_max_all[:, bass.ds(NT * b + NT, NT)],
                                          row_max[(k + 1) % 2][:]).then_inc(max_kept, 1)
                if here:
                    pool.wait_ge(inv_ready, b + 1)
                    nc.gpsimd.tensor_copy(inv_sum_all[:, bass.ds(NT * b, NT)], inv_sum[k][:]).then_inc(sum_kept, 1)
                    normalise(k, y_sb[k], moments_ready, NT * b + NT, var_ready, 2 * b + 2,
                              rstd_ready, b + 1, y_ready)

            slots(pool, slot)

            pool.wait_ge(off_known, 1)
            off = pool.value_load(off_int[0:1, 0:1], min_val=0, max_val=P)
            with pool.If(off > 0):
                with pool.Fori(0, B, 1) as b:
                    normalise(0, y_sb[0], g_moments, NT * b + NT, g_var, 2 * b + 2, g_rstd, b + 1, g_out)

        @block.tensor
        def _(pe):
            def transpose_x(b, k):
                pe.wait_ge(x_in[k], turn(b, k) + 16)
                if not isinstance(b, int) or b >= 2:
                    pe.wait_ge(masked_ready, NT * b - 2 * NT + 3)
                for t in range(NT):
                    last = nc.tensor.transpose(xT_bank(k)[:, t, :], x_sb[k][:, t, :], ident[:])
                last.then_inc(xT_done, 1)

            def score(b, k, t):
                if t == 0:
                    pe.wait_ge(xT_ready, 2 * b + 2)
                if t in (0, 2) and (not isinstance(b, int) or b > 0):
                    pe.wait_ge(masked_ready, NT * b - NT + t // 2 * 2 + 2)
                if t == 3:
                    pe.wait_ge(masked_ready, NT * b + 1)
                nc.tensor.matmul(score_bank(k, t)[:], xT[k % 2][:, t, :], xaT[k % 2][:],
                                 start=True, stop=True).then_inc(score_done, 1)

            def transpose_p(b, k2, t):
                pe.wait_ge(p_ready, NT * b + t + 1)
                for c in range(NT):
                    last = nc.tensor.transpose(pT_ps[t % 2][:, c, :], p_sb[k2][:, t, c, :], ident[:])
                last.then_inc(pT_done, 1)

            def weigh(b, k, t):
                pe.wait_ge(pT_ready, NT * b + t + 1)
                pe.wait_ge(o_free, NT * b + t + NT - 1)
                for c in range(NT):
                    last = nc.tensor.matmul(o_ps[t % 2][:], pT_sb[t][:, c, :], x_sb[k][:, c, :],
                                            start=(c == 0), stop=(c == NT - 1))
                last.then_inc(o_done, 1)

            def slot(b, k, here, next1, next2):
                for t in range(NT):
                    if next1:
                        score(b + 1, (k + 1) % XBUF, t)
                    if here:
                        transpose_p(b, k % 2, t)
                    if next2 and t == 1:
                        transpose_x(b + 2, (k + 2) % XBUF)
                    if here and t > 0:
                        weigh(b, k, t - 1)
                if here:
                    weigh(b, k, NT - 1)

            pe.wait_ge(ident_ready, 1)
            transpose_x(0, 0)
            slots(pe, slot)

            pe.wait_ge(off_ready, 2)
            nc.tensor.matmul(ring[0][0:1, 0:1], off_row[:], ones_col[:], start=True, stop=True).then_inc(off_sum, 1)
            pe.wait_ge(off_known, 1)
            off = pe.value_load(off_int[0:1, 0:1], min_val=0, max_val=P)
            with pe.If(off > 0):
                with pe.Fori(0, B, 1) as b:
                    pe.wait_ge(g_in, 32 * b + 32)
                    for t in range(NT):
                        last = nc.tensor.transpose(xT_bank(2)[:, t, :], x_sb[0][:, t, :], ident[:])
                    last.then_inc(g_xT_done, 1)
                    for r in range(R):
                        pe.wait_ge(g_xT_ready, b + 1)
                        pe.wait_ge(g_xa_ready, R * b + r + 1)
                        for t in range(NT):
                            if r > 0:
                                pe.wait_ge(g_e_ready, R * NT * b + NT * (r - 1) + t + 1)
                            nc.tensor.matmul(ring[t][:], xT[0][:, t, :], xaT[r % 2][:],
                                             start=True, stop=True).then_inc(g_score_done, 1)
                    for t in range(NT):
                        pe.wait_ge(g_p_ready, NT * b + t + 1)
                        for c in range(NT):
                            last = nc.tensor.transpose(pT_ps[t % 2][:, c, :], p_sb[0][:, t, c, :], ident[:])
                        last.then_inc(g_pT_done, 1)
                        pe.wait_ge(g_pT_ready, NT * b + t + 1)
                        if t >= 2:
                            pe.wait_ge(g_y, NT * b + t - 1)
                        for c in range(NT):
                            last = nc.tensor.matmul(o_ps[t % 2][:], pT_sb[t][:, c, :], x_sb[0][:, c, :],
                                                    start=(c == 0), stop=(c == NT - 1))
                        last.then_inc(g_o_done, 1)

        @block.scalar
        def _(act):
            act.dma_start(w_row[:], time_w[None, :].broadcast_to((P, T))).then_inc(const_in, 16)
            act.dma_start(t_row[:], t_rel.rearrange("r t -> (r t)")[None, :].broadcast_to((P, R * T))).then_inc(const_in, 16)
            with nc.allow_non_contiguous_dma(reason="five short columns"):
                act.dma_start(a_cols[:], a_rel.rearrange("r d -> d r")).then_inc(a_in, 16)
            act.wait_ge(angle_ready, 1)
            nc.scalar.activation(turns[:], theta[:], ACT.Sin).then_inc(cos_ready, 1)

            def copy_xT(b, k):
                act.wait_ge(xT_done, b + 1)
                nc.scalar.copy(xT[k % 2][:], xT_bank(k)).then_inc(xT_ready, 1)
                nc.scalar.mul(xaT[k % 2][:].rearrange("d (p t) -> d t p", t=NT), xT_bank(k),
                              a_scaled[:]).then_inc(xT_ready, 1)

            def exponents(b, k2, h):
                act.wait_ge(e_ready, 2 * b + h + 1)
                act.wait_ge(max_ready, 2 * b + h + 1)
                for t in (2 * h, 2 * h + 1):
                    nc.scalar.activation(p_sb[k2][:, t, :, :], e_sb[k2][:, t, :].rearrange("p (q c) -> p c q", c=NT),
                                         ACT.Exp, bias=neg_max[k2][:, t:t + 1], scale=BIG,
                                         accum_out=row_sum[k2][:, t:t + 1]).then_inc(p_ready, 1)

            def copy_pT(b, t):
                act.wait_ge(pT_done, NT * b + t + 1)
                nc.scalar.copy(pT_sb[t][:], pT_ps[t % 2][:]).then_inc(pT_ready, 1)

            def slot(b, k, here, next1, next2):
                for h in range(NT // 2):
                    if here:
                        copy_pT(b, 2 * h)
                        copy_pT(b, 2 * h + 1)
                    if next2 and h == 0:
                        copy_xT(b + 2, (k + 2) % XBUF)
                    if next1:
                        exponents(b + 1, (k + 1) % 2, h)

            act.wait_ge(a_ready, 1)
            copy_xT(0, 0)
            slots(act, slot)

            act.wait_ge(off_known, 1)
            off = act.value_load(off_int[0:1, 0:1], min_val=0, max_val=P)
            with act.If(off > 0):
                with act.Fori(0, B, 1) as b:
                    for u in range(R * NT):
                        r, t = divmod(u, NT)
                        act.wait_ge(g_score_done, R * NT * b + u + 1)
                        if u >= 2:
                            act.wait_ge(g_picked, R * NT * b + u - 1)
                        nc.scalar.activation(e_k[u % 2][:], ring[t][:], ACT.Identity,
                                             bias=c_rel[:, r:r + 1]).then_inc(g_e_ready, 1)
                    for t in range(NT):
                        act.wait_ge(g_neg_max, NT * b + t + 1)
                        nc.scalar.activation(p_sb[0][:, t, :, :], e_sb[0][:, t, :].rearrange("p (q c) -> p c q", c=NT),
                                             ACT.Exp, bias=neg_max[0][:, t:t + 1],
                                             accum_out=row_sum[0][:, t:t + 1]).then_inc(g_p_ready, 1)
                        act.wait_ge(g_pT_done, NT * b + t + 1)
                        nc.scalar.copy(pT_sb[t][:], pT_ps[t % 2][:]).then_inc(g_pT_ready, 1)

        @block.vector
        def _(dve):
            steps = [0]

            def angle(ins):
                steps[0] += 1
                ins.then_inc(angle_step, 1)
                dve.wait_ge(angle_step, steps[0])

            nc.vector.memset(ones_col[:], 1.0).then_inc(off_ready, 1)
            dve.sem_inc(o_free, NT)

            def constants():
                dve.wait_ge(const_in, 32)
                for r in range(R):
                    last = nc.vector.tensor_scalar(theta[:, r * T:(r + 1) * T], w_row[:], float(r + 1), None, ALU.mult)
                    if r < R - 1:
                        last.then_inc(angle_step, 1)
                        steps[0] += 1
                angle(last)
                angle(nc.vector.tensor_scalar(turns[:], theta[:], 1.0 / TWO_PI, ROUND, ALU.mult, ALU.add))
                angle(nc.vector.tensor_scalar(turns[:], turns[:], -ROUND, None, ALU.add))
                for part in (PI_A, PI_B, PI_C):
                    angle(nc.vector.scalar_tensor_tensor(theta[:], turns[:], -part, theta[:], ALU.mult, ALU.add))
                angle(nc.vector.scalar_tensor_tensor(turns[:], theta[:], -1.0, theta[:], ALU.mult, ALU.max))
                nc.vector.tensor_scalar(theta[:], turns[:], -1.0, TWO_PI / 4, ALU.mult, ALU.add).then_inc(angle_ready, 1)
                dve.wait_ge(a_in, 16)
                nc.vector.tensor_scalar(a_scaled[:], a_cols[:, 0:1], 1.0 / BIG, None, ALU.mult).then_inc(a_ready, 1)
                dve.wait_ge(cos_ready, 1)
                nc.vector.tensor_tensor(turns[:], turns[:], t_row[:], ALU.mult).then_inc(c_step, 1)
                dve.wait_ge(c_step, 1)
                nc.vector.reduce_sum(c_rel[:], turns[:].rearrange("p (r t) -> p r t", t=T), axis=AX.X).then_inc(c_ready, 1)
                dve.wait_ge(c_ready, 1)
                nc.vector.tensor_scalar(c_unit[:], c_rel[:, 0:1], 1.0 / BIG, None, ALU.mult).then_inc(c_ready, 1)
                dve.wait_ge(c_ready, 2)

            def make_mask(b, k):
                dve.wait_ge(adj_in[k], turn(b, k) + 16)
                nc.vector.tensor_scalar(mask_sb[k % 2][:], adj_sb[k][:], -1.0, c_unit[:], ALU.add,
                                        ALU.add).then_inc(mask_ready, 1)

            def mask_scores(b, k, t):
                k2 = k % 2
                if t == 0:
                    dve.wait_ge(mask_ready, b + 1)
                    if not isinstance(b, int) or b >= 2:
                        dve.wait_ge(max_kept, b)
                plain_wait(dve, score_done, NT * b + t + 1)
                nc.vector.tensor_tensor_reduce(out=e_sb[k2][:, t, :], in0=score_bank(k, t)[:], in1=mask_sb[k2][:, t, :],
                                               scale=1.0, scalar=-3.0e38, op0=ALU.add, op1=ALU.max,
                                               accum_out=row_max[k2][:, t:t + 1]).then_inc(masked_ready, 1)

            def leaky_relu(b, k2, h):
                rows = slice(2 * h, 2 * h + 2)
                dve.wait_ge(masked_ready, NT * b + 2 * h + 2)
                nc.vector.scalar_tensor_tensor(max_leaky[:, rows], row_max[k2][:, rows], SLOPE, row_max[k2][:, rows],
                                               ALU.mult, ALU.max).then_inc(max_leaky_ready, 1)
                e = e_sb[k2][:, rows, :]
                nc.vector.scalar_tensor_tensor(e, e, SLOPE, e, ALU.mult, ALU.max).then_inc(e_ready, 1)
                dve.wait_ge(max_leaky_ready, 2 * b + h + 1)
                nc.vector.tensor_scalar(neg_max[k2][:, rows], max_leaky[:, rows], -BIG, None,
                                        ALU.mult).then_inc(max_ready, 1)

            def invert_sums(b, k):
                dve.wait_ge(p_ready, NT * b + NT)
                nc.vector.reciprocal(inv_sum[k][:], row_sum[k % 2][:]).then_inc(inv_ready, 1)
                dve.wait_ge(stored[k], turn(b, k) + 16)
                dve.wait_ge(inv_ready, b + 1)

            def add_residual(b, k, t):
                dve.wait_ge(o_done, NT * b + t + 1)
                nc.vector.scalar_tensor_tensor(y_sb[k][:, t, :], o_ps[t % 2][:], inv_sum[k][:, t:t + 1],
                                               x_sb[k][:, t, :], ALU.mult, ALU.add).then_inc(o_free, 1)

            def moments(b, k, t):
                dve.wait_ge(o_free, NT * b + NT + t + 1)
                nc.vector.bn_stats(stats[k][:, t, :], y_sb[k][:, t, :]).then_inc(stats_ready, 1)

            def gather_moments(b, k):
                plain_wait(dve, stats_ready, NT * b + NT)
                for t in range(NT):
                    nc.vector.bn_aggr(mean_var[k][:, t, :], stats[k][:, t, :]).then_inc(moments_ready, 1)

            def slot(b, k, here, next1, next2):
                for h in range(NT // 2):
                    if next1:
                        mask_scores(b + 1, (k + 1) % XBUF, 2 * h)
                        mask_scores(b + 1, (k + 1) % XBUF, 2 * h + 1)
                        leaky_relu(b + 1, (k + 1) % 2, h)
                    if here and h == 0:
                        invert_sums(b, k)
                    if here:
                        add_residual(b, k, h)
                        moments(b, k, h)
                    if next2 and h == 0:
                        make_mask(b + 2, (k + 2) % XBUF)
                if here:
                    add_residual(b, k, 2)
                    moments(b, k, 2)
                    add_residual(b, k, 3)
                    moments(b, k, 3)
                    gather_moments(b, k)

            constants()
            make_mask(0, 0)
            slots(dve, slot)

            dve.wait_ge(max_kept, B)
            dve.wait_ge(sum_kept, B)
            low = -SCORE_MAX / BIG
            nc.vector.tensor_scalar(off_a[:], row_max_all[:], -0.5, None, ALU.is_gt).then_inc(off_step, 1)
            nc.vector.tensor_scalar(off_c[:], inv_sum_all[:], 1.0 / (N - 0.5), None, ALU.is_gt).then_inc(off_step, 1)
            dve.wait_ge(off_step, 2)
            nc.vector.tensor_tensor(off_c[:], off_c[:], off_a[:], ALU.is_gt).then_inc(off_step, 1)
            nc.vector.scalar_tensor_tensor(off_b[:], row_max_all[:], low, off_a[:], ALU.is_lt,
                                           ALU.mult).then_inc(off_step, 1)
            dve.wait_ge(off_step, 4)
            nc.vector.scalar_tensor_tensor(off_a[:], row_max_all[:], -low, off_b[:], ALU.is_gt,
                                           ALU.max).then_inc(off_step, 1)
            dve.wait_ge(off_step, 5)
            nc.vector.tensor_tensor(off_a[:], off_a[:], off_c[:], ALU.max).then_inc(off_step, 1)
            dve.wait_ge(off_step, 6)
            nc.vector.reduce_max(off_row[:], off_a[:], axis=AX.X).then_inc(off_ready, 1)
            dve.wait_ge(off_sum, 1)
            nc.vector.tensor_copy(off_int[:], ring[0][0:1, 0:1]).then_inc(off_known, 1)
            dve.wait_ge(off_known, 1)
            off = dve.value_load(off_int[0:1, 0:1], min_val=0, max_val=P)
            with dve.If(off > 0):
                with dve.Fori(0, B, 1) as b:
                    nc.vector.memset(e_sb[0][:], NEG).then_inc(g_fill, 1)
                    dve.wait_ge(g_xT_done, b + 1)
                    nc.vector.tensor_copy(xT[0][:], xT_bank(2)).then_inc(g_xT_ready, 1)
                    dve.wait_ge(g_xT_ready, b + 1)
                    dve.wait_ge(g_in, 32 * b + 32)
                    dve.wait_ge(g_fill, b + 1)
                    for r in range(R):
                        if r >= 2:
                            dve.wait_ge(g_score_done, R * NT * b + NT * (r - 1))
                        nc.vector.tensor_scalar(xaT[r % 2][:].rearrange("d (p t) -> d t p", t=NT), xT[0][:],
                                                a_cols[:, r:r + 1], None, ALU.mult).then_inc(g_xa_ready, 1)
                        for t in range(NT):
                            u = NT * r + t
                            nc.vector.tensor_scalar(hit[u % 2][:], adj_sb[0][:, t, :], float(r + 1), None,
                                                    ALU.is_equal).then_inc(g_hit, 1)
                            dve.wait_ge(g_e_ready, R * NT * b + u + 1)
                            nc.vector.scalar_tensor_tensor(leaky[u % 2][:], e_k[u % 2][:], SLOPE, e_k[u % 2][:],
                                                           ALU.mult, ALU.max).then_inc(g_hit, 1)
                            plain_wait(dve, g_hit, 2 * (R * NT * b + u) + 2)
                            nc.vector.copy_predicated(e_sb[0][:, t, :], hit[u % 2][:], leaky[u % 2][:]).then_inc(g_picked, 1)
                    for t in range(NT):
                        dve.wait_ge(g_picked, R * NT * b + NT * (R - 1) + t + 1)
                        nc.vector.reduce_max(row_max2[:, t:t + 1], e_sb[0][:, t, :], axis=AX.X).then_inc(g_max, 1)
                        dve.wait_ge(g_max, NT * b + t + 1)
                        nc.vector.tensor_scalar(neg_max[0][:, t:t + 1], row_max2[:, t:t + 1], -1.0, None,
                                                ALU.mult).then_inc(g_neg_max, 1)
                    dve.wait_ge(g_p_ready, NT * b + NT)
                    nc.vector.reciprocal(inv_sum[0][:], row_sum[0][:]).then_inc(g_inv, 1)
                    dve.wait_ge(g_inv, b + 1)
                    for t in range(NT):
                        dve.wait_ge(g_o_done, NT * b + t + 1)
                        nc.vector.scalar_tensor_tensor(y_sb[0][:, t, :], o_ps[t % 2][:], inv_sum[0][:, t:t + 1],
                                                       x_sb[0][:, t, :], ALU.mult, ALU.add).then_inc(g_y, 1)
                        dve.wait_ge(g_y, NT * b + t + 1)
                        nc.vector.bn_stats(stats[0][:, t, :], y_sb[0][:, t, :]).then_inc(g_stats, 1)
                        plain_wait(dve, g_stats, NT * b + t + 1)
                        nc.vector.bn_aggr(mean_var[0][:, t, :], stats[0][:, t, :]).then_inc(g_moments, 1)


_INS = ["x", "adj", "L0_gnn_a_rel", "L0_gnn_t_rel", "L0_gnn_time_w"]


def kernel(**inputs):
    import numpy as _np
    import concourse.bacc as _bacc
    from concourse import mybir as _mybir
    from concourse.bass_utils import run_bass_kernel_spmd as _run

    nc = _bacc.Bacc("TRN2", target_bir_lowering=False, num_devices=1)
    arrays, args = {}, []
    for name in _INS:
        a = _np.ascontiguousarray(inputs[name])
        arrays[f"in_{name}_dram"] = a
        args.append(nc.dram_tensor(f"in_{name}_dram", a.shape, _mybir.dt.from_np(a.dtype), kind="ExternalInput").ap())
    shape = inputs["x"].shape
    args.append(nc.dram_tensor("out_0_dram", shape, _mybir.dt.float32, kind="ExternalOutput").ap())
    gnn_resnorm_kernel(nc, *args)
    r = _run(nc, [arrays], core_ids=[0])
    return r.results[0]["out_0_dram"]
```

```python
import concourse.bass as bass
from concourse import mybir
from contextlib import ExitStack


def gnn_resnorm_kernel(
    nc: bass.Bass,
    x: bass.AP,
    adj: bass.AP,
    a_rel: bass.AP,
    t_rel: bass.AP,
    time_w: bass.AP,
    out: bass.AP,
):
    f32, f32r, i32, u8 = mybir.dt.float32, mybir.dt.float32r, mybir.dt.int32, mybir.dt.uint8
    ALU = mybir.AluOpType
    ACT = mybir.ActivationFunctionType
    AX = mybir.AxisListType

    B, N, D = x.shape
    R, T = t_rel.shape
    P = 128
    NT = N // P
    XBUF = 4
    WARM_UP = 7
    NEG = -9000000000000000.0
    SLOPE = 0.2
    EPS = 1e-5
    BIG = 2.0 ** 90
    SCORE_MAX = 1e15
    TWO_PI = 6.283185307179586
    PI_A = 6.28125
    PI_B = 0.0019350051879882812
    PI_C = TWO_PI - PI_A - PI_B
    ROUND = 1.5 * 2.0 ** 23

    x_v = x.rearrange("b (p t) d -> b p t d", t=NT)
    adj_v = adj.rearrange("b (p t) j -> b p t j", t=NT)
    out_v = out.rearrange("b (p t) d -> b p t d", t=NT)

    ctx = ExitStack()
    with ctx:
        def sb(name, shape, dt):
            return ctx.enter_context(nc.sbuf_tensor(name, shape, dt))

        def sem(name):
            return ctx.enter_context(nc.semaphore(name))

        ident = sb("ident", [P, P], f32)
        ones_col = sb("ones_col", [P, 1], f32)
        a_cols = sb("a_cols", [P, R], f32)
        a_scaled = sb("a_scaled", [P, 1], f32)
        w_row = sb("w_row", [P, T], f32)
        t_row = sb("t_row", [P, R * T], f32)
        theta = sb("theta", [P, R * T], f32)
        turns = sb("turns", [P, R * T], f32)
        c_rel = sb("c_rel", [P, R], f32)
        table = sb("table", [P, 2], f32)
        c_unit = sb("c_unit", [P, 1], f32)
        half_neg = sb("half_neg", [P, NT], f32)
        adj_sb = [sb(f"adj_sb{k}", [P, NT, N], i32) for k in range(XBUF)]
        x_sb = [sb(f"x_sb{k}", [P, NT, D], f32) for k in range(XBUF)]
        y_sb = [sb(f"y_sb{k}", [P, NT, D], f32) for k in range(XBUF)]
        mask_sb = [sb(f"mask_sb{k}", [P, NT, N], f32) for k in range(2)]
        whole = [sb(f"whole{k}", [P, 2, N], f32) for k in range(2)]
        high = [sb(f"high{k}", [P, 2, N], f32r) for k in range(2)]
        low = [sb(f"low{k}", [P, 2, N], f32r) for k in range(2)]
        e_sb = [sb(f"e_sb{k}", [P, NT, N], f32) for k in range(2)]
        p_sb = [sb(f"p_sb{k}", [P, NT, NT, P], f32) for k in range(2)]
        pT_sb = [sb(f"pT_sb{t}", [P, NT, P], f32) for t in range(NT)]
        row_max = [sb(f"row_max{k}", [P, NT], f32) for k in range(2)]
        row_max_all = sb("row_max_all", [P, B * NT], f32)
        max_leaky = sb("max_leaky", [P, NT], f32)
        neg_max = [sb(f"neg_max{k}", [P, NT], f32) for k in range(2)]
        row_sum = [sb(f"row_sum{k}", [P, NT], f32) for k in range(2)]
        inv_sum = [sb(f"inv_sum{k}", [P, NT], f32) for k in range(XBUF)]
        inv_sum_all = sb("inv_sum_all", [P, B * NT], f32)
        stats = [sb(f"stats{k}", [P, NT, 6], f32) for k in range(XBUF)]
        mean_var = [sb(f"mean_var{k}", [P, NT, 2], f32) for k in range(XBUF)]
        var_eps = [sb(f"var_eps{k}", [P, NT], f32) for k in range(XBUF)]
        rstd = [sb(f"rstd{k}", [P, NT], f32) for k in range(XBUF)]
        neg_mean = [sb(f"neg_mean{k}", [P, NT], f32) for k in range(XBUF)]
        off_a = sb("off_a", [P, B * NT], f32)
        off_b = sb("off_b", [P, B * NT], f32)
        off_c = sb("off_c", [P, B * NT], f32)
        off_row = sb("off_row", [P, 1], f32)
        off_int = sb("off_int", [1, 1], i32)
        row_max2 = sb("row_max2", [P, NT], f32)
        hit = [sb(f"hit{k}", [P, N], u8) for k in range(2)]
        leaky = [sb(f"leaky{k}", [P, N], f32) for k in range(2)]
        e_k = [sb(f"e_k{k}", [P, N], f32) for k in range(2)]

        ring = [ctx.enter_context(nc.psum_tensor(f"ring{n}", [P, N], f32)) for n in range(NT)]
        pT_ps = [ctx.enter_context(nc.psum_tensor(f"pT_ps{k}", [P, NT, P], f32)) for k in range(2)]
        o_ps = [ctx.enter_context(nc.psum_tensor(f"o_ps{k}", [P, D], f32)) for k in range(2)]

        def score_bank(k, t):
            return ring[(k + 1 + t) % NT]

        def xT(operand):
            return operand[:, 0, :].rearrange("d (t p) -> d t p", t=NT)

        def xaT(operand):
            return operand[:, 1, :]

        def xT_bank(k):
            return ring[(k - 1) % NT][:].rearrange("p (t q) -> p t q", t=NT)

        w_in = sem("w_in")
        t_in = sem("t_in")
        other_t_in = sem("other_t_in")
        a_in = sem("a_in")
        x_in = [sem(f"x_in{k}") for k in range(XBUF)]
        adj_in = [sem(f"adj_in{k}") for k in range(XBUF)]
        half_adj_in = sem("half_adj_in")
        ones_ready = sem("ones_ready")
        table_ready = sem("table_ready")
        a_ready = sem("a_ready")
        warm = sem("warm")
        passed = sem("passed")
        stored = [sem(f"stored{k}") for k in range(XBUF)]
        ident_zero = sem("ident_zero")
        ident_ready = sem("ident_ready")
        angle_step = sem("angle_step")
        angle_ready = sem("angle_ready")
        cos_ready = sem("cos_ready")
        c_step = sem("c_step")
        c_ready = sem("c_ready")
        half_mask_ready = sem("half_mask_ready")
        pool_mask_ready = sem("pool_mask_ready")
        mask_ready = sem("mask_ready")
        xT_done = sem("xT_done")
        xT_ready = sem("xT_ready")
        split_ready = sem("split_ready")
        score_done = sem("score_done")
        masked_ready = sem("masked_ready")
        e_ready = sem("e_ready")
        max_leaky_ready = sem("max_leaky_ready")
        max_ready = sem("max_ready")
        p_ready = sem("p_ready")
        pT_done = sem("pT_done")
        pT_ready = sem("pT_ready")
        o_done = sem("o_done")
        inv_ready = sem("inv_ready")
        o_free = sem("o_free")
        y_added = sem("y_added")
        stats_ready = sem("stats_ready")
        moments_ready = sem("moments_ready")
        var_ready = sem("var_ready")
        last_var_ready = sem("last_var_ready")
        rstd_ready = sem("rstd_ready")
        y_ready = sem("y_ready")
        max_kept = sem("max_kept")
        sum_kept = sem("sum_kept")
        off_step = sem("off_step")
        off_ready = sem("off_ready")
        off_sum = sem("off_sum")
        off_known = sem("off_known")
        g_in = sem("g_in")
        g_xT_done = sem("g_xT_done")
        g_xT_ready = sem("g_xT_ready")
        g_xa_ready = sem("g_xa_ready")
        g_score_done = sem("g_score_done")
        g_e_ready = sem("g_e_ready")
        g_hit = sem("g_hit")
        g_picked = sem("g_picked")
        g_fill = sem("g_fill")
        g_max = sem("g_max")
        g_neg_max = sem("g_neg_max")
        g_p_ready = sem("g_p_ready")
        g_pT_done = sem("g_pT_done")
        g_pT_ready = sem("g_pT_ready")
        g_o_done = sem("g_o_done")
        g_inv = sem("g_inv")
        g_y = sem("g_y")
        g_stats = sem("g_stats")
        g_moments = sem("g_moments")
        g_var = sem("g_var")
        g_rstd = sem("g_rstd")
        g_out = sem("g_out")
        g_stored = sem("g_stored")

        block = ctx.enter_context(nc.Block())

        LOOPED = B - XBUF

        def slots(engine, slot):
            slot(-1, 3, False, False, True, True)
            slot(0, 0, False, True, True, True)
            with engine.Fori(0, LOOPED // XBUF) as i:
                for n in range(1, XBUF + 1):
                    slot(XBUF * i + n, n % XBUF, True, True, True, True)
            for b in range(LOOPED + 1, B + 1):
                slot(b, b % XBUF, True, b < B, b + 1 < B, b + 2 < B)

        def turn(b, k):
            return 4 * (b - k)

        def plain_wait(engine, semaphore, value):
            engine.wait_ge(semaphore, value)
            engine.sem_inc(passed, 1)

        @block.sync
        def _(sp):
            def load_x(b, k):
                sp.dma_start(x_sb[k][:], x_v[bass.ds(b, 1)].rearrange("o p t d -> p (o t) d")).then_inc(x_in[k], 16)

            def load_adj(b, k):
                sp.dma_start(adj_sb[k][:], adj_v[bass.ds(b, 1)].rearrange("o p t j -> p (o t) j")).then_inc(adj_in[k], 16)

            def load_t(lo, hi, arrival):
                cols = t_rel[lo:hi, :].rearrange("r t -> (r t)")[None, :]
                sp.dma_start(t_row[:, lo * T:hi * T], cols.broadcast_to((P, (hi - lo) * T))).then_inc(arrival, 16)

            load_x(0, 0)
            sp.dma_start(w_row[:], time_w[None, :].broadcast_to((P, T))).then_inc(w_in, 16)
            load_t(0, 1, t_in)
            half = NT // 2
            sp.dma_start(adj_sb[0][:, :half], adj_v[0][:, :half]).then_inc(half_adj_in, 16)
            load_x(1, 1)
            sp.dma_start(adj_sb[0][:, half:], adj_v[0][:, half:]).then_inc(adj_in[0], 16)
            for k in range(1, XBUF):
                if k + 1 < XBUF:
                    load_x(k + 1, k + 1)
                load_adj(k, k)
            load_t(1, R, other_t_in)
            for k in range(XBUF):
                sp.sem_inc(stored[k], 16)

            def store(b, k):
                plain_wait(sp, y_ready, NT * b + NT)
                sp.dma_start(out_v[bass.ds(b, 1)].rearrange("o p t d -> p (o t) d"), y_sb[k][:]).then_inc(stored[k], 16)

            def step(j, k, adj_next, x_next, done):
                if adj_next:
                    if isinstance(j, int) and j == 1:
                        sp.wait_ge(pool_mask_ready, 1)
                    plain_wait(sp, mask_ready, j + 1)
                    load_adj(j + XBUF, k)
                if x_next:
                    plain_wait(sp, y_added, j)
                    load_x(j - 1 + XBUF, (k - 1) % XBUF)
                if done:
                    store(j - 2, (k - 2) % XBUF)

            step(0, 0, True, False, False)
            step(1, 1, True, True, False)
            with sp.Fori(0, LOOPED // XBUF - 1) as i:
                for n in range(2, XBUF + 2):
                    step(XBUF * i + n, n % XBUF, True, True, True)
            for j in range(LOOPED - 2, B + 1):
                step(j, j % XBUF, j < LOOPED, j <= LOOPED, True)
            last = XBUF - 1
            for rows, ready in ((slice(0, half), half), (slice(half, NT), NT)):
                sp.wait_ge(y_ready, NT * (B - 1) + ready)
                sp.dma_start(out_v[B - 1][:, rows], y_sb[last][:, rows]).then_inc(stored[last], 16)
            for k in range(XBUF):
                sp.wait_ge(stored[k], 16 * (B // XBUF + 1) + (16 if k == last else 0))

            sp.wait_ge(off_known, 1)
            off = sp.value_load(off_int[0:1, 0:1], min_val=0, max_val=P)
            with sp.If(off > 0):
                with sp.Fori(0, B, 1) as b:
                    sp.dma_start(x_sb[0][:], x_v[bass.ds(b, 1)].rearrange("o p t d -> p (o t) d")).then_inc(g_in, 16)
                    sp.dma_start(adj_sb[0][:], adj_v[bass.ds(b, 1)].rearrange("o p t j -> p (o t) j")).then_inc(g_in, 16)
                    plain_wait(sp, g_out, NT * b + NT)
                    sp.dma_start(out_v[bass.ds(b, 1)].rearrange("o p t d -> p (o t) d"), y_sb[0][:]).then_inc(g_stored, 16)
                    plain_wait(sp, g_stored, 16 * b + 16)

        @block.gpsimd
        def _(pool):
            nc.gpsimd.memset(ident[:], 0.0).then_inc(ident_zero, 1)
            nc.gpsimd.memset(half_neg[:], -0.5).then_inc(ident_zero, 1)
            pool.wait_ge(ident_zero, 2)
            nc.gpsimd.affine_select(out=ident[:], in_=ident[:], compare_op=ALU.not_equal, fill=1.0, base=0,
                                    pattern=[[-1, P]], channel_multiplier=1).then_inc(ident_ready, 1)

            def split(b, k2):
                pool.wait_ge(xT_ready, 4 * b + 2)
                nc.gpsimd.tensor_tensor(low[k2][:], whole[k2][:], high[k2][:], ALU.subtract).then_inc(split_ready, 1)

            def root(k, var, var_at, done):
                pool.wait_ge(var, var_at)
                nc.gpsimd.tensor_tensor(rstd[k][:], var_eps[k][:], half_neg[:], ALU.pow).then_inc(done, 1)

            def root_terms(k, moments, moments_at, var):
                plain_wait(pool, moments, moments_at)
                nc.gpsimd.tensor_scalar(var_eps[k][:], mean_var[k][:, :, 1], EPS, None, ALU.add).then_inc(var, 1)
                nc.gpsimd.tensor_scalar(neg_mean[k][:], mean_var[k][:, :, 0], -1.0, None, ALU.mult).then_inc(var, 1)

            def normalise(k, ready, ready_at, done):
                plain_wait(pool, ready, ready_at)
                for t in range(NT):
                    nc.gpsimd.tensor_scalar(y_sb[k][:, t, :], y_sb[k][:, t, :], neg_mean[k][:, t:t + 1],
                                            rstd[k][:, t:t + 1], ALU.add, ALU.mult).then_inc(done, 1)

            def slot(b, k, prev, here, next1, next2):
                kp = (k - 1) % XBUF
                if prev and next1:
                    pool.wait_ge(inv_ready, b)
                    nc.gpsimd.tensor_copy(inv_sum_all[:, bass.ds(NT * b - NT, NT)], inv_sum[kp][:]).then_inc(sum_kept, 1)
                    pool.wait_ge(o_free, NT * b + NT)
                    nc.gpsimd.tensor_tensor(y_sb[kp][:], y_sb[kp][:], x_sb[kp][:], ALU.add).then_inc(y_added, 1)
                if next2:
                    split(b + 2, (k + 2) % 2)
                if next2 and not here:
                    pool.wait_ge(c_ready, 2)
                    pool.wait_ge(adj_in[1], 16)
                    nc.gpsimd.tensor_scalar(mask_sb[1][:, NT // 2:], adj_sb[1][:, NT // 2:], -1.0, c_unit[:],
                                            ALU.add, ALU.add).then_inc(pool_mask_ready, 1)
                if prev and here:
                    root_terms(kp, moments_ready, NT * b, var_ready)
                    root(kp, var_ready, 2 * b, rstd_ready)
                if prev and not here:
                    root(kp, last_var_ready, 2, rstd_ready)
                if prev and next1:
                    normalise(kp, rstd_ready, b, y_ready)
                if next1 and next2:
                    pool.wait_ge(masked_ready, NT * b + 2 * NT)
                    nc.gpsimd.tensor_copy(row_max_all[:, bass.ds(NT * b + NT, NT)],
                                          row_max[(k + 1) % 2][:]).then_inc(max_kept, 1)

            slots(pool, slot)

            pool.wait_ge(off_known, 1)
            off = pool.value_load(off_int[0:1, 0:1], min_val=0, max_val=P)
            with pool.If(off > 0):
                with pool.Fori(0, B, 1) as b:
                    root_terms(0, g_moments, NT * b + NT, g_var)
                    root(0, g_var, 2 * b + 2, g_rstd)
                    normalise(0, g_rstd, b + 1, g_out)

        @block.tensor
        def _(pe):
            def transpose_x(b, k):
                pe.wait_ge(x_in[k], turn(b, k) + 16)
                if not isinstance(b, int) or b >= 2:
                    pe.wait_ge(masked_ready, NT * b - 2 * NT + 1)
                for t in range(NT):
                    last = nc.tensor.transpose(xT_bank(k)[:, t, :], x_sb[k][:, t, :], ident[:])
                last.then_inc(xT_done, 1)

            def score(b, k, t):
                first = isinstance(b, int) and b == 0
                if t == 0 and first:
                    pe.wait_ge(xT_ready, 2)
                elif t == 0:
                    pe.wait_ge(split_ready, b)
                if t < NT - 1 and (not isinstance(b, int) or b > 0):
                    pe.wait_ge(masked_ready, NT * b - NT + t + 2)
                if t == NT - 1 and (not isinstance(b, int) or b + 1 < B):
                    pe.wait_ge(xT_ready, 4 * b + 6)
                if first:
                    nc.tensor.matmul(score_bank(k, t)[:], xT(whole[k])[:, t, :], xaT(whole[k]),
                                     start=True, stop=True).then_inc(score_done, 1)
                else:
                    hi, lo = high[k % 2], low[k % 2]
                    nc.tensor.matmul(score_bank(k, t)[:], xT(lo)[:, t, :], xaT(hi), start=True, stop=False)
                    nc.tensor.matmul(score_bank(k, t)[:], xT(hi)[:, t, :], xaT(lo), start=False, stop=False)
                    nc.tensor.matmul(score_bank(k, t)[:], xT(hi)[:, t, :], xaT(hi),
                                     start=False, stop=True).then_inc(score_done, 1)

            def transpose_p(b, k2, t):
                pe.wait_ge(p_ready, NT * b + t + 1)
                for c in range(NT):
                    last = nc.tensor.transpose(pT_ps[t % 2][:, c, :], p_sb[k2][:, t, c, :], ident[:])
                last.then_inc(pT_done, 1)

            def weigh(b, k, t):
                pe.wait_ge(pT_ready, NT * b + t + 1)
                pe.wait_ge(o_free, NT * b + t + NT - 1)
                for c in range(NT):
                    last = nc.tensor.matmul(o_ps[t % 2][:], pT_sb[t][:, c, :], x_sb[k][:, c, :],
                                            start=(c == 0), stop=(c == NT - 1))
                last.then_inc(o_done, 1)

            def slot(b, k, prev, here, next1, next2):
                if here and next2:
                    transpose_x(b + 2, (k + 2) % XBUF)
                for t in range(NT):
                    if here and t == 0:
                        transpose_p(b, k % 2, 0)
                    if next2 and not here and t == 1:
                        transpose_x(b + 2, (k + 2) % XBUF)
                    if next1:
                        score(b + 1, (k + 1) % XBUF, t)
                    if here:
                        if t + 1 < NT:
                            transpose_p(b, k % 2, t + 1)
                        weigh(b, k, t)

            pe.wait_ge(ident_ready, 1)
            transpose_x(0, 0)
            for n in range(WARM_UP):
                last = nc.tensor.transpose(pT_ps[1][:, 0, :], ident[:], ident[:])
            last.then_inc(warm, 1)
            slots(pe, slot)

            pe.wait_ge(off_ready, 1)
            nc.tensor.matmul(ring[0][0:1, 0:1], off_row[:], ones_col[:], start=True, stop=True).then_inc(off_sum, 1)
            pe.wait_ge(off_known, 1)
            off = pe.value_load(off_int[0:1, 0:1], min_val=0, max_val=P)
            with pe.If(off > 0):
                with pe.Fori(0, B, 1) as b:
                    pe.wait_ge(g_in, 32 * b + 32)
                    for t in range(NT):
                        last = nc.tensor.transpose(xT_bank(2)[:, t, :], x_sb[0][:, t, :], ident[:])
                    last.then_inc(g_xT_done, 1)
                    for r in range(R):
                        pe.wait_ge(g_xT_ready, b + 1)
                        pe.wait_ge(g_xa_ready, R * b + r + 1)
                        for t in range(NT):
                            if r > 0:
                                pe.wait_ge(g_e_ready, R * NT * b + NT * (r - 1) + t + 1)
                            nc.tensor.matmul(ring[t][:], xT(whole[0])[:, t, :], xaT(whole[r % 2]),
                                             start=True, stop=True).then_inc(g_score_done, 1)
                    for t in range(NT):
                        pe.wait_ge(g_p_ready, NT * b + t + 1)
                        for c in range(NT):
                            last = nc.tensor.transpose(pT_ps[t % 2][:, c, :], p_sb[0][:, t, c, :], ident[:])
                        last.then_inc(g_pT_done, 1)
                        pe.wait_ge(g_pT_ready, NT * b + t + 1)
                        if t >= 2:
                            pe.wait_ge(g_y, NT * b + t - 1)
                        for c in range(NT):
                            last = nc.tensor.matmul(o_ps[t % 2][:], pT_sb[t][:, c, :], x_sb[0][:, c, :],
                                                    start=(c == 0), stop=(c == NT - 1))
                        last.then_inc(g_o_done, 1)

        @block.scalar
        def _(act):
            with nc.allow_non_contiguous_dma(reason="five short columns"):
                act.dma_start(a_cols[:], a_rel.rearrange("r d -> d r")).then_inc(a_in, 16)

            def scale_xT(b, k):
                act.wait_ge(xT_done, b + 1)
                nc.scalar.mul(xaT(whole[k % 2]).rearrange("d (p t) -> d t p", t=NT), xT_bank(k),
                              a_scaled[:]).then_inc(xT_ready, 1)

            def copy_xT(k):
                nc.scalar.copy(xT(whole[k % 2]), xT_bank(k)).then_inc(xT_ready, 1)

            def high_xT(k):
                nc.scalar.copy(xT(high[k % 2]), xT_bank(k)).then_inc(xT_ready, 1)

            def high_xaT(k):
                nc.scalar.mul(xaT(high[k % 2]).rearrange("d (p t) -> d t p", t=NT), xT_bank(k),
                              a_scaled[:]).then_inc(xT_ready, 1)

            def exponents(b, k2, t):
                if t % 2 == 0:
                    act.wait_ge(e_ready, 2 * b + t // 2 + 1)
                    act.wait_ge(max_ready, 2 * b + t // 2 + 1)
                nc.scalar.activation(p_sb[k2][:, t, :, :], e_sb[k2][:, t, :].rearrange("p (q c) -> p c q", c=NT),
                                     ACT.Exp, bias=neg_max[k2][:, t:t + 1], scale=BIG,
                                     accum_out=row_sum[k2][:, t:t + 1]).then_inc(p_ready, 1)

            def copy_pT(b, t):
                act.wait_ge(pT_done, NT * b + t + 1)
                nc.scalar.copy(pT_sb[t][:], pT_ps[t % 2][:]).then_inc(pT_ready, 1)

            def divide(b, k, t):
                act.wait_ge(o_done, NT * b + t + 1)
                if t == 0:
                    act.wait_ge(inv_ready, b + 1)
                    act.wait_ge(stored[k], turn(b, k) + 16)
                nc.scalar.mul(y_sb[k][:, t, :], o_ps[t % 2][:], inv_sum[k][:, t:t + 1]).then_inc(o_free, 1)

            def slot(b, k, prev, here, next1, next2):
                if prev and here:
                    divide(b - 1, (k - 1) % XBUF, 3)
                if next2:
                    scale_xT(b + 2, (k + 2) % XBUF)
                if here:
                    copy_pT(b, 0)
                if next2:
                    copy_xT((k + 2) % XBUF)
                if here:
                    if not next1:
                        copy_pT(b, 1)
                    exponents(b, k % 2, 2)
                    if next1:
                        copy_pT(b, 1)
                    exponents(b, k % 2, 3)
                if next2:
                    high_xT((k + 2) % XBUF)
                if here:
                    copy_pT(b, 2)
                if here and next1:
                    divide(b, k, 0)
                if next2:
                    high_xaT((k + 2) % XBUF)
                if here and next1:
                    divide(b, k, 1)
                if here:
                    copy_pT(b, 3)
                if next1:
                    exponents(b + 1, (k + 1) % 2, 0)
                    exponents(b + 1, (k + 1) % 2, 1)
                if here and next1:
                    divide(b, k, 2)

            def cosines(n, lo, hi):
                act.wait_ge(angle_ready, n)
                nc.scalar.activation(turns[:, lo * T:hi * T], theta[:, lo * T:hi * T], ACT.Sin).then_inc(cos_ready, 1)

            act.sem_inc(o_free, NT)
            act.wait_ge(ones_ready, 1)
            nc.scalar.activation(table[:, 0:1], ones_col[:], ACT.Sin).then_inc(table_ready, 1)
            act.wait_ge(a_ready, 1)
            scale_xT(0, 0)
            copy_xT(0)
            cosines(1, 0, 1)
            nc.scalar.activation(table[:, 1:2], ones_col[:], ACT.Exp).then_inc(table_ready, 1)
            slots(act, slot)

            act.wait_ge(off_known, 1)
            off = act.value_load(off_int[0:1, 0:1], min_val=0, max_val=P)
            with act.If(off > 0):
                cosines(2, 1, R)
                act.wait_ge(c_ready, 3)
                with act.Fori(0, B, 1) as b:
                    for u in range(R * NT):
                        r, t = divmod(u, NT)
                        act.wait_ge(g_score_done, R * NT * b + u + 1)
                        if u >= 2:
                            act.wait_ge(g_picked, R * NT * b + u - 1)
                        nc.scalar.activation(e_k[u % 2][:], ring[t][:], ACT.Identity,
                                             bias=c_rel[:, r:r + 1]).then_inc(g_e_ready, 1)
                    for t in range(NT):
                        act.wait_ge(g_neg_max, NT * b + t + 1)
                        nc.scalar.activation(p_sb[0][:, t, :, :], e_sb[0][:, t, :].rearrange("p (q c) -> p c q", c=NT),
                                             ACT.Exp, bias=neg_max[0][:, t:t + 1],
                                             accum_out=row_sum[0][:, t:t + 1]).then_inc(g_p_ready, 1)
                        act.wait_ge(g_pT_done, NT * b + t + 1)
                        nc.scalar.copy(pT_sb[t][:], pT_ps[t % 2][:]).then_inc(g_pT_ready, 1)

        @block.vector
        def _(dve):
            steps = [0]

            def angle(ins):
                steps[0] += 1
                ins.then_inc(angle_step, 1)
                dve.wait_ge(angle_step, steps[0])

            nc.vector.memset(ones_col[:], 1.0).then_inc(ones_ready, 1)

            def type_terms(n, lo, hi):
                cols = slice(lo * T, hi * T)
                a, q = theta[:, cols], turns[:, cols]
                for r in range(lo, hi):
                    steps[0] += 1
                    nc.vector.tensor_scalar(theta[:, r * T:(r + 1) * T], w_row[:], float(r + 1), None,
                                            ALU.mult).then_inc(angle_step, 1)
                dve.wait_ge(angle_step, steps[0])
                angle(nc.vector.tensor_scalar(q, a, 1.0 / TWO_PI, ROUND, ALU.mult, ALU.add))
                angle(nc.vector.tensor_scalar(q, q, -ROUND, None, ALU.add))
                for part in (PI_A, PI_B, PI_C):
                    angle(nc.vector.scalar_tensor_tensor(a, q, -part, a, ALU.mult, ALU.add))
                angle(nc.vector.scalar_tensor_tensor(q, a, -1.0, a, ALU.mult, ALU.max))
                nc.vector.tensor_scalar(a, q, -1.0, TWO_PI / 4, ALU.mult, ALU.add).then_inc(angle_ready, 1)
                dve.wait_ge(t_in if lo == 0 else other_t_in, 16)
                dve.wait_ge(cos_ready, n)
                nc.vector.tensor_tensor(q, q, t_row[:, cols], ALU.mult).then_inc(c_step, 1)
                dve.wait_ge(c_step, n)
                nc.vector.reduce_sum(c_rel[:, lo:hi], q.rearrange("p (r t) -> p r t", t=T), axis=AX.X).then_inc(c_ready, 1)

            def make_mask(b, k):
                dve.wait_ge(adj_in[k], turn(b, k) + 16)
                nc.vector.tensor_scalar(mask_sb[k % 2][:], adj_sb[k][:], -1.0, c_unit[:], ALU.add,
                                        ALU.add).then_inc(mask_ready, 1)

            def mask_scores(b, k, t):
                k2 = k % 2
                if isinstance(b, int) and b == 0 and t < NT // 2:
                    dve.wait_ge(half_mask_ready, 1)
                else:
                    dve.wait_ge(mask_ready, b + 1)
                if isinstance(b, int) and b == 1 and t >= NT // 2:
                    dve.wait_ge(pool_mask_ready, 1)
                if t == 0:
                    if not isinstance(b, int) or b >= 2:
                        dve.wait_ge(max_kept, b - 1)
                plain_wait(dve, score_done, NT * b + t + 1)
                nc.vector.tensor_tensor_reduce(out=e_sb[k2][:, t, :], in0=score_bank(k, t)[:], in1=mask_sb[k2][:, t, :],
                                               scale=1.0, scalar=-3.0e38, op0=ALU.add, op1=ALU.max,
                                               accum_out=row_max[k2][:, t:t + 1]).then_inc(masked_ready, 1)

            def leaky_relu(b, k2, h):
                rows = slice(2 * h, 2 * h + 2)
                dve.wait_ge(masked_ready, NT * b + 2 * h + 2)
                nc.vector.scalar_tensor_tensor(max_leaky[:, rows], row_max[k2][:, rows], SLOPE, row_max[k2][:, rows],
                                               ALU.mult, ALU.max).then_inc(max_leaky_ready, 1)
                e = e_sb[k2][:, rows, :]
                nc.vector.scalar_tensor_tensor(e, e, SLOPE, e, ALU.mult, ALU.max).then_inc(e_ready, 1)
                dve.wait_ge(max_leaky_ready, 2 * b + h + 1)
                nc.vector.tensor_scalar(neg_max[k2][:, rows], max_leaky[:, rows], -BIG, None,
                                        ALU.mult).then_inc(max_ready, 1)

            def invert_sums(b, k):
                dve.wait_ge(p_ready, NT * b + NT)
                nc.vector.reciprocal(inv_sum[k][:], row_sum[k % 2][:]).then_inc(inv_ready, 1)

            def row_stats(b, k):
                dve.wait_ge(y_added, b + 1)
                for t in range(NT):
                    nc.vector.bn_stats(stats[k][:, t, :], y_sb[k][:, t, :]).then_inc(stats_ready, 1)

            def last_stats(b, k, t):
                dve.wait_ge(o_free, NT * b + NT + t + 1)
                nc.vector.bn_stats(stats[k][:, t, :], y_sb[k][:, t, :]).then_inc(stats_ready, 1)

            def moments(b, k, lo=0, hi=NT):
                plain_wait(dve, stats_ready, NT * b + hi)
                for t in range(lo, hi):
                    nc.vector.bn_aggr(mean_var[k][:, t, :], stats[k][:, t, :]).then_inc(moments_ready, 1)

            def residual(b, k, t):
                dve.wait_ge(o_done, NT * b + t + 1)
                nc.vector.scalar_tensor_tensor(y_sb[k][:, t, :], o_ps[t % 2][:], inv_sum[k][:, t:t + 1],
                                               x_sb[k][:, t, :], ALU.mult, ALU.add).then_inc(o_free, 1)

            def normalise(b, k):
                dve.wait_ge(rstd_ready, b + 1)
                for t in range(NT):
                    nc.vector.tensor_scalar(y_sb[k][:, t, :], y_sb[k][:, t, :], neg_mean[k][:, t:t + 1],
                                            rstd[k][:, t:t + 1], ALU.add, ALU.mult).then_inc(y_ready, 1)

            def last_slot(b, k):
                kept = slice(NT * b, NT * b + NT)
                nc.vector.tensor_copy(row_max_all[:, kept], row_max[k % 2][:]).then_inc(off_step, 1)
                nc.vector.tensor_copy(inv_sum_all[:, NT * b - NT:NT * b], inv_sum[k - 1][:]).then_inc(off_step, 1)
                dve.wait_ge(o_free, NT * b + NT)
                nc.vector.tensor_tensor(y_sb[k - 1][:], y_sb[k - 1][:], x_sb[k - 1][:], ALU.add).then_inc(y_added, 1)
                dve.wait_ge(max_kept, b)
                dve.wait_ge(off_step, 2)
                lowest = -SCORE_MAX / BIG
                nc.vector.tensor_scalar(off_a[:], row_max_all[:], -0.5, None, ALU.is_gt).then_inc(off_step, 1)
                dve.wait_ge(off_step, 3)
                nc.vector.scalar_tensor_tensor(off_b[:], row_max_all[:], lowest, off_a[:], ALU.is_lt,
                                               ALU.mult).then_inc(off_step, 1)
                dve.wait_ge(off_step, 4)
                nc.vector.scalar_tensor_tensor(off_b[:], row_max_all[:], -lowest, off_b[:], ALU.is_gt,
                                               ALU.max).then_inc(off_step, 1)
                row_stats(b - 1, k - 1)
                invert_sums(b, k)
                nc.vector.reciprocal(inv_sum_all[:, kept], row_sum[k % 2][:]).then_inc(off_step, 1)
                dve.wait_ge(inv_ready, b + 1)
                dve.wait_ge(stored[k], turn(b, k) + 16)
                residual(b, k, 0)
                residual(b, k, 1)
                moments(b - 1, k - 1)
                dve.wait_ge(sum_kept, b - 1)
                dve.wait_ge(off_step, 6)
                nc.vector.tensor_scalar(off_c[:], inv_sum_all[:], 1.0 / (N - 0.5), None, ALU.is_gt).then_inc(off_step, 1)
                residual(b, k, 2)
                last_stats(b, k, 0)
                last_stats(b, k, 1)
                dve.wait_ge(off_step, 7)
                nc.vector.tensor_tensor(off_c[:], off_c[:], off_a[:], ALU.is_gt).then_inc(off_step, 1)
                dve.wait_ge(off_step, 8)
                nc.vector.tensor_tensor(off_a[:], off_b[:], off_c[:], ALU.max).then_inc(off_step, 1)
                last_stats(b, k, 2)
                dve.wait_ge(off_step, 9)
                nc.vector.reduce_max(off_row[:], off_a[:], axis=AX.X).then_inc(off_ready, 1)
                moments(b, k, 0, 3)
                residual(b, k, 3)
                last_stats(b, k, 3)
                moments(b, k, 3, 4)
                dve.wait_ge(moments_ready, NT * b + NT)
                nc.vector.tensor_scalar(var_eps[k][:], mean_var[k][:, :, 1], EPS, None, ALU.add).then_inc(last_var_ready, 1)
                nc.vector.tensor_scalar(neg_mean[k][:], mean_var[k][:, :, 0], -1.0, None, ALU.mult).then_inc(last_var_ready, 1)
                normalise(b - 1, k - 1)
                dve.wait_ge(off_sum, 1)
                nc.vector.tensor_copy(off_int[:], ring[0][0:1, 0:1]).then_inc(off_known, 1)
                normalise(b, k)

            def first_slot():
                mask_scores(0, 0, 0)
                mask_scores(0, 0, 1)
                leaky_relu(0, 0, 0)
                dve.wait_ge(adj_in[0], 16)
                nc.vector.tensor_scalar(mask_sb[0][:, NT // 2:], adj_sb[0][:, NT // 2:], -1.0, c_unit[:], ALU.add,
                                        ALU.add).then_inc(mask_ready, 1)
                mask_scores(0, 0, 2)
                mask_scores(0, 0, 3)
                leaky_relu(0, 0, 1)
                dve.wait_ge(adj_in[1], 16)
                nc.vector.tensor_scalar(mask_sb[1][:, :NT // 2], adj_sb[1][:, :NT // 2], -1.0, c_unit[:], ALU.add,
                                        ALU.add).then_inc(mask_ready, 1)

            def slot(b, k, prev, here, next1, next2):
                if not prev and not here:
                    first_slot()
                    return
                if not here and prev:
                    return
                if next1:
                    mask_scores(b + 1, (k + 1) % XBUF, 0)
                if next2:
                    make_mask(b + 2, (k + 2) % XBUF)
                if here and not prev:
                    invert_sums(b, k)
                if prev and here and not next1:
                    last_slot(b, k)
                    return
                if next1:
                    mask_scores(b + 1, (k + 1) % XBUF, 1)
                if here and prev:
                    invert_sums(b, k)
                if next1:
                    leaky_relu(b + 1, (k + 1) % 2, 0)
                    mask_scores(b + 1, (k + 1) % XBUF, 2)
                if prev:
                    row_stats(b - 1, (k - 1) % XBUF)
                if next1:
                    mask_scores(b + 1, (k + 1) % XBUF, 3)
                if prev and next2:
                    moments(b - 1, (k - 1) % XBUF)
                if next1:
                    leaky_relu(b + 1, (k + 1) % 2, 1)
                if prev and not next2:
                    moments(b - 1, (k - 1) % XBUF)

            dve.wait_ge(a_in, 16)
            nc.vector.tensor_scalar(a_scaled[:], a_cols[:, 0:1], 1.0 / BIG, None, ALU.mult).then_inc(a_ready, 1)
            dve.wait_ge(w_in, 16)
            type_terms(1, 0, 1)
            dve.wait_ge(c_ready, 1)
            nc.vector.tensor_scalar(c_unit[:], c_rel[:, 0:1], 1.0 / BIG, None, ALU.mult).then_inc(c_ready, 1)
            dve.wait_ge(c_ready, 2)
            dve.wait_ge(half_adj_in, 16)
            nc.vector.tensor_scalar(mask_sb[0][:, :NT // 2], adj_sb[0][:, :NT // 2], -1.0, c_unit[:], ALU.add,
                                    ALU.add).then_inc(half_mask_ready, 1)
            slots(dve, slot)

            dve.wait_ge(off_known, 1)
            off = dve.value_load(off_int[0:1, 0:1], min_val=0, max_val=P)
            with dve.If(off > 0):
                type_terms(2, 1, R)
                with dve.Fori(0, B, 1) as b:
                    nc.vector.memset(e_sb[0][:], NEG).then_inc(g_fill, 1)
                    dve.wait_ge(g_xT_done, b + 1)
                    nc.vector.tensor_copy(xT(whole[0]), xT_bank(2)).then_inc(g_xT_ready, 1)
                    dve.wait_ge(g_xT_ready, b + 1)
                    dve.wait_ge(g_in, 32 * b + 32)
                    dve.wait_ge(g_fill, b + 1)
                    for r in range(R):
                        if r >= 2:
                            dve.wait_ge(g_score_done, R * NT * b + NT * (r - 1))
                        nc.vector.tensor_scalar(xaT(whole[r % 2]).rearrange("d (p t) -> d t p", t=NT), xT(whole[0]),
                                                a_cols[:, r:r + 1], None, ALU.mult).then_inc(g_xa_ready, 1)
                        for t in range(NT):
                            u = NT * r + t
                            nc.vector.tensor_scalar(hit[u % 2][:], adj_sb[0][:, t, :], float(r + 1), None,
                                                    ALU.is_equal).then_inc(g_hit, 1)
                            dve.wait_ge(g_e_ready, R * NT * b + u + 1)
                            nc.vector.scalar_tensor_tensor(leaky[u % 2][:], e_k[u % 2][:], SLOPE, e_k[u % 2][:],
                                                           ALU.mult, ALU.max).then_inc(g_hit, 1)
                            plain_wait(dve, g_hit, 2 * (R * NT * b + u) + 2)
                            nc.vector.copy_predicated(e_sb[0][:, t, :], hit[u % 2][:], leaky[u % 2][:]).then_inc(g_picked, 1)
                    for t in range(NT):
                        dve.wait_ge(g_picked, R * NT * b + NT * (R - 1) + t + 1)
                        nc.vector.reduce_max(row_max2[:, t:t + 1], e_sb[0][:, t, :], axis=AX.X).then_inc(g_max, 1)
                        dve.wait_ge(g_max, NT * b + t + 1)
                        nc.vector.tensor_scalar(neg_max[0][:, t:t + 1], row_max2[:, t:t + 1], -1.0, None,
                                                ALU.mult).then_inc(g_neg_max, 1)
                    dve.wait_ge(g_p_ready, NT * b + NT)
                    nc.vector.reciprocal(inv_sum[0][:], row_sum[0][:]).then_inc(g_inv, 1)
                    dve.wait_ge(g_inv, b + 1)
                    for t in range(NT):
                        dve.wait_ge(g_o_done, NT * b + t + 1)
                        nc.vector.scalar_tensor_tensor(y_sb[0][:, t, :], o_ps[t % 2][:], inv_sum[0][:, t:t + 1],
                                                       x_sb[0][:, t, :], ALU.mult, ALU.add).then_inc(g_y, 1)
                        dve.wait_ge(g_y, NT * b + t + 1)
                        nc.vector.bn_stats(stats[0][:, t, :], y_sb[0][:, t, :]).then_inc(g_stats, 1)
                        plain_wait(dve, g_stats, NT * b + t + 1)
                        nc.vector.bn_aggr(mean_var[0][:, t, :], stats[0][:, t, :]).then_inc(g_moments, 1)


_INS = ["x", "adj", "L0_gnn_a_rel", "L0_gnn_t_rel", "L0_gnn_time_w"]


def kernel(**inputs):
    import numpy as _np
    import concourse.bacc as _bacc
    from concourse import mybir as _mybir
    from concourse.bass_utils import run_bass_kernel_spmd as _run

    nc = _bacc.Bacc("TRN2", target_bir_lowering=False, num_devices=1)
    arrays, args = {}, []
    for name in _INS:
        a = _np.ascontiguousarray(inputs[name])
        arrays[f"in_{name}_dram"] = a
        args.append(nc.dram_tensor(f"in_{name}_dram", a.shape, _mybir.dt.from_np(a.dtype), kind="ExternalInput").ap())
    shape = inputs["x"].shape
    args.append(nc.dram_tensor("out_0_dram", shape, _mybir.dt.float32, kind="ExternalOutput").ap())
    gnn_resnorm_kernel(nc, *args)
    r = _run(nc, [arrays], core_ids=[0])
    return r.results[0]["out_0_dram"]
```
